# Optimizing a Trainium2 kernel written in Bass

```python
import numpy as np
import jax
import jax.numpy as jnp

def _softmax(x, axis=-1):
    return jax.nn.softmax(x, axis=axis)

def _gelu(x):
    return jax.nn.gelu(x, approximate=True)

def _silu(x):
    return jax.nn.silu(x)

def _sigmoid(x):
    return jax.nn.sigmoid(x)

def _layernorm(x, axis=-1, eps=1e-05):
    m = jnp.mean(x, axis=axis, keepdims=True)
    v = jnp.var(x, axis=axis, keepdims=True)
    return (x - m) / jnp.sqrt(v + eps)

def _scatter_add(tgt, idx, src, axis=0):
    return tgt.at[idx].add(src)

def _segment_sum(src, seg, n):
    return jax.ops.segment_sum(src, seg, n)
kernel_name = 'mk_early_fusion_d1_tok_img4096_r4_01d379'

def setup_inputs(seed: int=0):
    np.random.seed(seed)
    _w = jnp.asarray

    def _rec_inputs():
        import jax
        import jax.numpy as jnp
        _rk = jax.random.key(seed)
        x = -0.00348982 + 0.707501 * jax.random.normal(jax.random.fold_in(_rk, 1), (4, 128, 64, 2), jnp.float32)
        txt = 6.73332e-06 + 0.02 * jax.random.normal(jax.random.fold_in(_rk, 2), (4, 512, 1024), jnp.float32)
        return (x, txt)
    x, txt = _rec_inputs()

    def _L0_tok_setup():
        import jax, jax.numpy as jnp
        import numpy as np
        H, N, S, CH, LEN = (128, 64, 128, 1, 1024)

        def _s4d_kernel(log_dt, C, B, inv_A_real, A_imag, L):
            dt = jnp.exp(log_dt)
            Cc = C[..., 0] + 1j * C[..., 1]
            Bc = B[..., 0] + 1j * B[..., 1]
            A = -jnp.exp(inv_A_real) + 1j * A_imag
            rep = H // A.shape[0]
            A = jnp.tile(A, (rep, 1))
            Bc = jnp.tile(Bc, (rep, 1))
            dtA = A * dt[:, None]
            Cc = Bc[None, :, :] * Cc
            Cc = Cc * (jnp.exp(dtA) - 1.0) / A
            ell = jnp.arange(L, dtype=jnp.float32)
            V = jnp.exp(dtA[:, :, None] * ell)
            K = 2.0 * jnp.einsum('chn,hnl->chl', Cc, V).real
            return K.astype(jnp.float32)
        key = jax.random.key(seed)
        k1, k2 = jax.random.split(key, 2)
        log_dt = jax.random.uniform(k1, (H,), minval=float(np.log(0.001)), maxval=float(np.log(0.1))).astype(jnp.float32)
        inv_A_real = jnp.full((S, N), float(np.log(0.5)), dtype=jnp.float32)
        A_imag = jnp.tile((np.pi * jnp.arange(N, dtype=jnp.float32))[None, :], (S, 1))
        B = jnp.stack([jnp.ones((S, N), jnp.float32), jnp.zeros((S, N), jnp.float32)], axis=-1)
        C = (jax.random.normal(k2, (CH, H, N, 2)) * 0.5 ** 0.5).astype(jnp.float32)
        return {'log_dt': log_dt, 'C': C, 'B': B, 'inv_A_real': inv_A_real, 'A_imag': A_imag, 'L': LEN}
    _L0_tok_all = _L0_tok_setup()
    _L0_tok_in = {k: v for k, v in _L0_tok_all.items() if k in ('log_dt', 'B', 'inv_A_real', 'A_imag')}
    del _L0_tok_all

    def _L0_attn_setup():
        import jax, jax.numpy as jnp
        import numpy as np
        H = 1024
        D = 2048
        N = 16
        K = 4
        R = 64
        BATCH = 1
        L = 512
        EPS = 1e-06

        def _rmsnorm(x, w):
            return x * jax.lax.rsqrt(jnp.mean(x * x, axis=-1, keepdims=True) + EPS) * w
        key = jax.random.key(seed)
        ks = jax.random.split(key, 10)
        s = 0.02
        return {'hidden_states': jax.random.normal(ks[0], (BATCH, L, H), jnp.float32), 'W_in': jax.random.normal(ks[1], (2 * D, H), jnp.float32) * s, 'conv_w': jax.random.normal(ks[2], (D, K), jnp.float32) * s, 'conv_b': jax.random.normal(ks[3], (D,), jnp.float32) * s, 'Wx': jax.random.normal(ks[4], (R + 2 * N, D), jnp.float32) * s, 'dt_ln_w': jnp.ones((R,), jnp.float32), 'b_ln_w': jnp.ones((N,), jnp.float32), 'c_ln_w': jnp.ones((N,), jnp.float32), 'Wdt': jax.random.normal(ks[5], (D, R), jnp.float32) * s, 'dt_bias': jax.random.normal(ks[6], (D,), jnp.float32) * s, 'A': -jnp.exp(jax.random.normal(ks[7], (D, N), jnp.float32) * 0.5), 'D_param': jnp.ones((D,), jnp.float32), 'W_out': jax.random.normal(ks[8], (H, D), jnp.float32) * s}
    _L0_attn_all = _L0_attn_setup()
    _L0_attn_in = {k: v for k, v in _L0_attn_all.items() if k in ('W_in', 'conv_w', 'conv_b', 'Wx', 'dt_ln_w', 'b_ln_w', 'c_ln_w', 'Wdt', 'dt_bias', 'A', 'D_param', 'W_out')}
    del _L0_attn_all

    def _L0_ffn_setup():
        import jax, jax.numpy as jnp
        import numpy as np
        IN_F = 1024
        OUT_F = 1024
        RANK = 8
        NUM_EXPERTS = 64
        TOP_K = 16
        ROUTER_DIM = 16
        ALPHA = 32
        SCALING = ALPHA / TOP_K
        BOTTLENECK = NUM_EXPERTS * RANK
        key = jax.random.key(seed)
        ks = jax.random.split(key, 5)
        x = jax.random.normal(ks[0], (4, 1024, IN_F), dtype=jnp.float32)
        bound_a = float(np.sqrt(6.0 / IN_F))
        A_w = jax.random.uniform(ks[1], (BOTTLENECK, IN_F), jnp.float32, -bound_a, bound_a)
        B_w = jax.random.normal(ks[2], (OUT_F, BOTTLENECK), dtype=jnp.float32) * 0.02
        Wq_w = jax.random.normal(ks[3], (ROUTER_DIM, IN_F), dtype=jnp.float32) * 0.02
        keys = jax.random.normal(ks[4], (NUM_EXPERTS, ROUTER_DIM), dtype=jnp.float32) * 0.01
        return {'x': x, 'A_w': A_w, 'B_w': B_w, 'Wq_w': Wq_w, 'keys': keys}
    _L0_ffn_all = _L0_ffn_setup()
    _L0_ffn_in = {k: v for k, v in _L0_ffn_all.items() if k in ('A_w', 'B_w', 'Wq_w', 'keys')}
    del _L0_ffn_all
    return {'x': x, 'txt': txt, 'L0_tok_log_dt': _L0_tok_in['log_dt'], 'L0_tok_B': _L0_tok_in['B'], 'L0_tok_inv_A_real': _L0_tok_in['inv_A_real'], 'L0_tok_A_imag': _L0_tok_in['A_imag'], 'L0_attn_W_in': _L0_attn_in['W_in'], 'L0_attn_conv_w': _L0_attn_in['conv_w'], 'L0_attn_conv_b': _L0_attn_in['conv_b'], 'L0_attn_Wx': _L0_attn_in['Wx'], 'L0_attn_dt_ln_w': _L0_attn_in['dt_ln_w'], 'L0_attn_b_ln_w': _L0_attn_in['b_ln_w'], 'L0_attn_c_ln_w': _L0_attn_in['c_ln_w'], 'L0_attn_Wdt': _L0_attn_in['Wdt'], 'L0_attn_dt_bias': _L0_attn_in['dt_bias'], 'L0_attn_A': _L0_attn_in['A'], 'L0_attn_D_param': _L0_attn_in['D_param'], 'L0_attn_W_out': _L0_attn_in['W_out'], 'L0_ffn_A_w': _L0_ffn_in['A_w'], 'L0_ffn_B_w': _L0_ffn_in['B_w'], 'L0_ffn_Wq_w': _L0_ffn_in['Wq_w'], 'L0_ffn_keys': _L0_ffn_in['keys']}

def reference(x, txt, L0_tok_log_dt, L0_tok_B, L0_tok_inv_A_real, L0_tok_A_imag, L0_attn_W_in, L0_attn_conv_w, L0_attn_conv_b, L0_attn_Wx, L0_attn_dt_ln_w, L0_attn_b_ln_w, L0_attn_c_ln_w, L0_attn_Wdt, L0_attn_dt_bias, L0_attn_A, L0_attn_D_param, L0_attn_W_out, L0_ffn_A_w, L0_ffn_B_w, L0_ffn_Wq_w, L0_ffn_keys):
    import jax
    import jax.numpy as jnp

    def _L0_tok_ref(log_dt, C, B, inv_A_real, A_imag, L):
        import jax, jax.numpy as jnp
        import numpy as np
        H, N, S, CH, LEN = (128, 64, 128, 1, 1024)

        def _s4d_kernel(log_dt, C, B, inv_A_real, A_imag, L):
            dt = jnp.exp(log_dt)
            Cc = C[..., 0] + 1j * C[..., 1]
            Bc = B[..., 0] + 1j * B[..., 1]
            A = -jnp.exp(inv_A_real) + 1j * A_imag
            rep = H // A.shape[0]
            A = jnp.tile(A, (rep, 1))
            Bc = jnp.tile(Bc, (rep, 1))
            dtA = A * dt[:, None]
            Cc = Bc[None, :, :] * Cc
            Cc = Cc * (jnp.exp(dtA) - 1.0) / A
            ell = jnp.arange(L, dtype=jnp.float32)
            V = jnp.exp(dtA[:, :, None] * ell)
            K = 2.0 * jnp.einsum('chn,hnl->chl', Cc, V).real
            return K.astype(jnp.float32)
        return _s4d_kernel(log_dt, C, B, inv_A_real, A_imag, L)

    def _L0_attn_ref(hidden_states, W_in, conv_w, conv_b, Wx, dt_ln_w, b_ln_w, c_ln_w, Wdt, dt_bias, A, D_param, W_out):
        import jax, jax.numpy as jnp
        import numpy as np
        H = 1024
        D = 2048
        N = 16
        K = 4
        R = 64
        BATCH = 1
        L = 512
        EPS = 1e-06

        def _rmsnorm(x, w):
            return x * jax.lax.rsqrt(jnp.mean(x * x, axis=-1, keepdims=True) + EPS) * w
        proj = hidden_states @ W_in.T
        u, gate = jnp.split(proj, 2, axis=-1)
        x = jnp.transpose(u, (0, 2, 1))
        x = jax.lax.conv_general_dilated(x, conv_w[:, None, :], window_strides=(1,), padding=[(K - 1, 0)], dimension_numbers=('NCH', 'OIH', 'NCH'), feature_group_count=D)
        u = jax.nn.silu(jnp.transpose(x, (0, 2, 1)) + conv_b)
        ssm_p = u @ Wx.T
        dt, Bm, Cm = jnp.split(ssm_p, [R, R + N], axis=-1)
        dt = _rmsnorm(dt, dt_ln_w)
        Bm = _rmsnorm(Bm, b_ln_w)
        Cm = _rmsnorm(Cm, c_ln_w)
        delta = jax.nn.softplus(dt @ Wdt.T + dt_bias)

        def step(state, xs):
            d_t, B_t, C_t, u_t = xs
            dA = jnp.exp(d_t[..., None] * A)
            state = dA * state + (d_t * u_t)[..., None] * B_t[:, None, :]
            y_t = jnp.einsum('bdn,bn->bd', state, C_t)
            return (state, y_t)
        init = jnp.zeros((hidden_states.shape[0], D, N), hidden_states.dtype)
        xs = (jnp.swapaxes(delta, 0, 1), jnp.swapaxes(Bm, 0, 1), jnp.swapaxes(Cm, 0, 1), jnp.swapaxes(u, 0, 1))
        _, ys = jax.lax.scan(step, init, xs)
        y = jnp.swapaxes(ys, 0, 1) + u * D_param
        y = y * jax.nn.silu(gate)
        return y @ W_out.T

    def _L0_ffn_ref(x, A_w, B_w, Wq_w, keys):
        import jax, jax.numpy as jnp
        import numpy as np
        IN_F = 1024
        OUT_F = 1024
        RANK = 8
        NUM_EXPERTS = 64
        TOP_K = 16
        ROUTER_DIM = 16
        ALPHA = 32
        SCALING = ALPHA / TOP_K
        BOTTLENECK = NUM_EXPERTS * RANK
        q = jnp.einsum('bsd,rd->bsr', x, Wq_w)
        scores = jnp.einsum('bsr,er->bse', q, keys)
        top_vals, top_idx = jax.lax.top_k(scores, TOP_K)
        top_w = jax.nn.softmax(top_vals, axis=-1)
        gate = jnp.sum(jax.nn.one_hot(top_idx, NUM_EXPERTS, dtype=top_w.dtype) * top_w[..., None], axis=-2)
        z = jnp.einsum('bsd,nd->bsn', x, A_w)
        z = z.reshape(*z.shape[:-1], NUM_EXPERTS, RANK)
        z_gated = (z * gate[..., None]).reshape(*z.shape[:-2], BOTTLENECK)
        out = jnp.einsum('bsn,on->bso', z_gated, B_w) * SCALING
        return out
    h = _L0_tok_ref(L0_tok_log_dt, x, L0_tok_B, L0_tok_inv_A_real, L0_tok_A_imag, 1024)
    h = jnp.concatenate([h, txt], axis=1)
    h = h + _L0_attn_ref(_layernorm(h, axis=-1), L0_attn_W_in, L0_attn_conv_w, L0_attn_conv_b, L0_attn_Wx, L0_attn_dt_ln_w, L0_attn_b_ln_w, L0_attn_c_ln_w, L0_attn_Wdt, L0_attn_dt_bias, L0_attn_A, L0_attn_D_param, L0_attn_W_out)
    h = h + _L0_ffn_ref(_layernorm(h, axis=-1), L0_ffn_A_w, L0_ffn_B_w, L0_ffn_Wq_w, L0_ffn_keys)
    return h

_drawn_inputs = setup_inputs


def setup_inputs(seed=0):
    import zlib

    import numpy as np

    out = dict(_drawn_inputs(seed))
    spreads = {'L0_tok_inv_A_real': (-0.6931471824645996, 0.2),
     'L0_attn_dt_ln_w': (1.0, 0.2),
     'L0_attn_b_ln_w': (1.0, 0.2),
     'L0_attn_c_ln_w': (1.0, 0.2),
     'L0_attn_D_param': (1.0, 0.2)}
    factors = {}
    for name, (base, spread) in spreads.items():
        noise = np.random.default_rng([zlib.crc32(name.encode()), seed]).standard_normal(out[name].shape)
        drawn = base * np.exp(spread * noise) if base else spread * noise
        out[name] = jnp.asarray(drawn.astype(out[name].dtype))
    for name, factor in factors.items():
        out[name] = (out[name] * factor).astype(out[name].dtype)
    return out
```

```python
import numpy as np
from contextlib import ExitStack

import concourse.bass as bass
from concourse import mybir

P = 128
F32 = mybir.dt.float32
ALU = mybir.AluOpType
ACT = mybir.ActivationFunctionType
AX = mybir.AxisListType.X

B = 4
HS, NS = 128, 64
L = 1024
KC = L // P
TOK = 640
TT = TOK // P
HALF = TOK // 2
D = 2048
DC = D // P
N = 16
R = 64
RBC = R + 2 * N
TAPS = 4
E = 64
RANK = 8
RD = 16
BN = E * RANK
MC = BN // P

NA, NB1, NB2 = 16, 8, 8
NV = NA + NB1 + NB2
TWO_PI_HI = 6.28125
TWO_PI_MID = 0.0019350051879882812
TWO_PI_LO = 2 * np.pi - TWO_PI_HI - TWO_PI_MID
ROUND = 1.5 * 2.0 ** 23
PI_MAX = 3.1415925
LN_EPS = 1e-5
RMS_EPS = 1e-6


def tokens_part(nc, a, sem):
    with ExitStack() as ctx:
        sb = lambda name, shape: ctx.enter_context(nc.sbuf_tensor(name, shape, F32))
        cst = sb("t_cst", [P, NV + 8])
        aim, iar, br, bi, ldt = (sb(f"t_{x}", [P, HS]) for x in ("aim", "iar", "br", "bi", "ldt"))
        cr, ci = sb("t_cr", [P, B, HS]), sb("t_ci", [P, B, HS])
        small = {x: sb(f"t_s_{x}", [P, HS]) for x in (
            "are", "dt", "zr", "zi", "den", "rden", "inr", "ini", "nr", "p0", "p1", "mr", "mi", "gr", "gi", "gb", "gbn")}
        two = sb("t_two", [P, 2, HS, NV])
        th, kk = two[:, 0], two[:, 1]
        mag = sb("t_mag", [P, HS, NV])
        own, swp = sb("t_own", [P, HS, NV]), sb("t_swp", [P, HS, NV])
        h_re, h_im, h_sg = (sb(f"t_h{x}", [P, HS, NB2]) for x in ("re", "im", "sg"))
        e2 = sb("t_e2", [P, HS, NB1 * NB2])
        q_own, q_swp, q_tmp = (sb(f"t_q{x}", [P, HS, NA]) for x in ("own", "swp", "tmp"))
        ca, cb = sb("t_ca", [P, HS, B]), sb("t_cb", [P, HS, B])
        w = sb("t_w", [P, HS, B * NA])
        tmp = two[:].rearrange("p x h v -> p (x h v)").rearrange("p (h v) -> p h v", h=HS)
        kout = mag[:].rearrange("p h v -> p (h v)").rearrange("p (h v) -> p h v", h=HS // 2)
        ps = [ctx.enter_context(nc.psum_tensor(f"t_ps{g}", [P, 8, 64], F32)) for g in range(8)]
        ld, dv, ac, mm, ev, st = (sem(f"t_{x}") for x in ("ld", "dv", "ac", "mm", "ev", "st"))
        marks = {}
        block = ctx.enter_context(nc.Block())

        lv = cst[:, 0:NV]
        ph = [cst[:, NV:NV + 1], cst[:, NV + 1:NV + 2]]
        ph2pi = [cst[:, NV + 2:NV + 3], cst[:, NV + 3:NV + 4]]
        sgn, nsgn = cst[:, NV + 4:NV + 5], cst[:, NV + 5:NV + 6]

        def over_v(x, n):
            return x.unsqueeze(2).broadcast_to([P, HS, n])

        @block.sync
        def _(sp):
            n = 0
            for half in range(2):
                rows = slice(64 * half, 64 * half + 64)
                for dst, src in ((aim, a["aimT"]), (iar, a["iarT"]), (br, a["brT"]), (bi, a["biT"])):
                    sp.dma_start(dst[rows, :], src).then_inc(ld, 16)
                sp.dma_start(cr[rows, :, :], a["crT"]).then_inc(ld, 16)
                sp.dma_start(ci[rows, :, :], a["ciT"]).then_inc(ld, 16)
                n += 6
            sp.dma_start(ldt[:, :], a["log_dt"].partition_broadcast(P)).then_inc(ld, 16)
            sp.dma_start(cst[:, :], a["cst"]).then_inc(ld, 16)
            assert n + 2 == 14
            sp.wait_ge(ev, 8)
            for hh in range(2):
                for c in range(B):
                    p0 = 64 * hh + NA * c
                    dst = a["h_all"][c, 64 * hh:64 * hh + 64, :].rearrange("h (a b) -> a h b", a=NA)
                    sp.dma_start(dst, kout[p0:p0 + NA, :, :]).then_inc(st, 16)
            for c in range(B):
                sp.dma_start(a["h_all"][c, P:TOK, :], a["txt"][c]).then_inc(st, 16)
            sp.wait_ge(st, 16 * 12)

        count = [0]
        marks_mag = 4
        marks_arg = (11, 18)

        @block.scalar
        def _(act):
            act.wait_ge(ld, 16 * 14)
            act.activation(small["dt"][:], ldt[:], ACT.Exp).then_inc(ac, 1)
            act.activation(small["are"][:], iar[:], ACT.Exp).then_inc(ac, 1)
            act.wait_ge(dv, marks_mag)
            act.activation(mag[:], mag[:], ACT.Exp).then_inc(ac, 1)
            for x, (t, m) in enumerate(((own, marks_arg[0]), (swp, marks_arg[1]))):
                act.wait_ge(dv, m)
                act.activation(t[:], t[:], ACT.Sin).then_inc(ac, 1)

        @block.vector
        def _(dve):
            def link(ins):
                count[0] += 1
                ins.then_inc(dv, 1)
                dve.wait_ge(dv, count[0])

            s = small
            dve.wait_ge(ac, 2)
            dve.wait_ge(ld, 16 * 14)
            link(dve.scalar_tensor_tensor(out=s["zr"][:], in0=s["are"][:], scalar=-1.0, in1=s["dt"][:],
                                          op0=ALU.mult, op1=ALU.mult))
            link(dve.tensor_tensor(s["zi"][:], aim[:], s["dt"][:], ALU.mult))
            lvb = lv.unsqueeze(1).broadcast_to([P, HS, NV])
            link(dve.tensor_tensor(th, over_v(s["zi"][:], NV), lvb, ALU.mult))
            link(dve.tensor_tensor(mag[:], over_v(s["zr"][:], NV), lvb, ALU.mult))
            assert count[0] == marks_mag
            for x, t in enumerate((own, swp)):
                link(dve.tensor_scalar(kk, th, float(1 / (2 * np.pi)), ph[x], ALU.mult, ALU.add))
                link(dve.tensor_scalar(kk, kk, ROUND, -ROUND, ALU.add, ALU.add))
                link(dve.scalar_tensor_tensor(out=t[:], in0=kk, scalar=-TWO_PI_HI, in1=th, op0=ALU.mult, op1=ALU.add))
                link(dve.scalar_tensor_tensor(out=t[:], in0=kk, scalar=-TWO_PI_MID, in1=t[:], op0=ALU.mult, op1=ALU.add))
                link(dve.scalar_tensor_tensor(out=t[:], in0=kk, scalar=-TWO_PI_LO, in1=t[:], op0=ALU.mult, op1=ALU.add))
                link(dve.tensor_scalar(t[:], t[:], ph2pi[x], PI_MAX, ALU.add, ALU.min))
                link(dve.tensor_scalar(t[:], t[:], -PI_MAX, None, ALU.max))
                assert count[0] == marks_arg[x]
            for x, t in enumerate((own, swp)):
                dve.wait_ge(ac, 4 + x)
                link(dve.tensor_tensor(t[:], t[:], mag[:], ALU.mult))
            lo, hi = slice(0, 64), slice(64, P)
            v2 = slice(NA + NB1, NV)
            for dst, first, second in ((h_re, own, swp), (h_im, swp, own)):
                link(dve.tensor_copy(dst[lo, :, :], first[lo, :, v2]))
                link(dve.tensor_copy(dst[hi, :, :], second[hi, :, v2]))
            link(dve.tensor_scalar(h_sg[:], h_im[:], nsgn, None, ALU.mult))
            shape = [P, HS, NB1, NB2]
            e2v = e2[:].rearrange("p h (x y) -> p h x y", x=NB1)
            tmpv = tmp.rearrange("p h (x y) -> p h x y", x=NB1)
            b1 = slice(NA, NA + NB1)
            link(dve.tensor_tensor(e2v, own[:, :, b1].unsqueeze(3).broadcast_to(shape),
                                   h_re[:].unsqueeze(2).broadcast_to(shape), ALU.mult))
            link(dve.tensor_tensor(tmpv, swp[:, :, b1].unsqueeze(3).broadcast_to(shape),
                                   h_sg[:].unsqueeze(2).broadcast_to(shape), ALU.mult))
            link(dve.tensor_tensor(e2[:], e2[:], tmp, ALU.add))
            tt = lambda o, x, y, op: link(dve.tensor_tensor(s[o][:], x, y, op))
            tt("den", s["are"][:], s["are"][:], ALU.mult)
            tt("p0", aim[:], aim[:], ALU.mult)
            tt("den", s["den"][:], s["p0"][:], ALU.add)
            link(dve.reciprocal(s["rden"][:], s["den"][:]))
            link(dve.scalar_tensor_tensor(out=s["inr"][:], in0=s["are"][:], scalar=-1.0, in1=s["rden"][:],
                                          op0=ALU.mult, op1=ALU.mult))
            link(dve.scalar_tensor_tensor(out=s["ini"][:], in0=aim[:], scalar=-1.0, in1=s["rden"][:],
                                          op0=ALU.mult, op1=ALU.mult))
            link(dve.tensor_scalar(s["nr"][:], h_re[:, :, 1], -1.0, None, ALU.add))
            ni = h_im[:, :, 1]

            def complex_product(ore, oim, xr, xi, yr, yi):
                tt("p0", xr, yr, ALU.mult)
                tt("p1", xi, yi, ALU.mult)
                tt(ore, s["p0"][:], s["p1"][:], ALU.subtract)
                tt("p0", xr, yi, ALU.mult)
                tt("p1", xi, yr, ALU.mult)
                tt(oim, s["p0"][:], s["p1"][:], ALU.add)

            complex_product("mr", "mi", s["nr"][:], ni, s["inr"][:], s["ini"][:])
            complex_product("gr", "gi", br[:], bi[:], s["mr"][:], s["mi"][:])
            link(dve.tensor_scalar(s["gr"][:], s["gr"][:], 2.0, None, ALU.mult))
            link(dve.tensor_scalar(s["gb"][:], s["gi"][:], nsgn, 2.0, ALU.mult, ALU.mult))
            link(dve.tensor_scalar(s["gbn"][:], s["gb"][:], -1.0, None, ALU.mult))
            va = slice(0, NA)
            for dst, first, second, g2 in ((q_own, own, swp, "gb"), (q_swp, swp, own, "gbn")):
                link(dve.tensor_tensor(dst[:], first[:, :, va], over_v(s["gr"][:], NA), ALU.mult))
                link(dve.tensor_tensor(q_tmp[:], second[:, :, va], over_v(s[g2][:], NA), ALU.mult))
                link(dve.tensor_tensor(dst[:], dst[:], q_tmp[:], ALU.add))
            link(dve.tensor_scalar(ca[:].rearrange("p h c -> p c h"), cr[:], sgn, None, ALU.mult))
            link(dve.tensor_scalar(cb[:].rearrange("p h c -> p c h"), ci[:], -1.0, None, ALU.mult))
            shape = [P, HS, B, NA]
            wv = w[:].rearrange("p h (c x) -> p h c x", c=B)
            tmpw = tmp.rearrange("p h (c x) -> p h c x", c=B)
            link(dve.tensor_tensor(wv, q_own[:].unsqueeze(2).broadcast_to(shape),
                                   ca[:].unsqueeze(3).broadcast_to(shape), ALU.mult))
            link(dve.tensor_tensor(tmpw, q_swp[:].unsqueeze(2).broadcast_to(shape),
                                   cb[:].unsqueeze(3).broadcast_to(shape), ALU.mult))
            link(dve.tensor_tensor(w[:], w[:], tmp, ALU.add))
            marks["w"] = count[0]
            for g in range(8):
                dve.wait_ge(mm, g + 1)
                dve.tensor_copy(kout[:, 8 * g:8 * g + 8, :], ps[g][:]).then_inc(ev, 1)

        @block.tensor
        def _(pe):
            pe.wait_ge(dv, marks["w"])
            for g in range(8):
                for x in range(8):
                    for hh in range(2):
                        h = 64 * hh + 8 * g + x
                        last = pe.matmul(ps[g][64 * hh:64 * hh + 64, x, :], w[:, h, :], e2[:, h, :],
                                         start=True, stop=True)
                last.then_inc(mm, 1)


CREDIT = 4
DMA = 16
RING_A, RING_U, RING_H, RING_C = 4, 2, 2, 2


def done(count):
    return count + CREDIT


def stored(count):
    return DMA * count + DMA


def over_chunks(eng, body):
    with eng.Fori(0, DC // 2 - 1) as c2:
        for place in range(2):
            body(2 * c2 + place, place, c2, False)
    for place in range(2):
        body(DC - 2 + place, place, DC // 2 - 1, place == 1)


def row(t, i):
    return t[bass.ds(i, 1)].squeeze(0)


def mixer_part(nc, a, sem):
    with ExitStack() as ctx:
        sb = lambda name, shape: ctx.enter_context(nc.sbuf_tensor(name, shape, F32))
        pair = lambda name: [sem(f"{name}{x}") for x in range(2)]

        b_bc, c_bc = sb("b_bc", [P, N, TOK]), sb("c_bc", [P, N, TOK])
        xnT = sb("xnT", [P, 2, KC, TOK])
        decay = sb("decay", [P, RING_A, TOK])
        drive = sb("drive", [P, RING_U, TOK])
        state = sb("state", [P, RING_H, TOK])
        prod = sb("prod", [P, RING_C, TOK])
        u_new = sb("u_new", [P, TOK])
        raw = sb("raw", [P, TAPS - 1 + TOK])
        u_y = sb("u_y", [P, 2, TOK])
        delta = sb("delta", [P, 2, TOK])
        du = sb("du", [P, 2, TOK])
        s_gate = sb("s_gate", [P, TOK])
        sp_tmp = sb("sp_tmp", [P, TOK])
        ssmT = sb("ssmT", [RBC, TOK])
        w_u = sb("w_u_sb", [P, 2, KC, P])
        w_g = sb("w_g_sb", [P, 2, KC, P])
        w_dt = sb("w_dt_sb", [R, 2, P])
        w_x = sb("w_x_sb", [P, DC * RBC])
        a_par = sb("a_par", [P, DC * N])
        conv_w = sb("conv_w_sb", [P, DC * TAPS])
        vec = sb("vec", [P, 3 * DC])
        conv_b, dt_bias, d_par = (vec[:, DC * x:DC * x + DC] for x in range(3))
        ln_w = sb("ln_w", [P, RBC])
        ident = sb("ident_sb", [P, P])
        h_t = sb("h_t", [P, L])
        stats = sb("stats", [P, 2, 6])
        mv = sb("mv", [P, 4])
        ssm = sb("ssm", [P, TT, RBC])
        ssm_ms = sb("ssm_ms", [P, 3, TT])
        inv_count = sb("inv_count", [P, 3, TT])
        consts = sb("consts", [P, 3])
        zero = sb("zero", [1, TT * RBC])

        bank_pair = lambda name: ctx.enter_context(nc.psum_tensor(name, [P, 2, 512], F32))
        y_ps, g0, g1 = bank_pair("y_ps"), bank_pair("g0"), bank_pair("g1")
        ssm_ps = ctx.enter_context(nc.psum_tensor("ssm_ps", [P, 512], F32))

        cst_ld, ht_ld, bc_st = sem("cst_ld"), sem("ht_ld"), sem("bc_st")
        wu_ld, wg_ld, wdt_ld, uy_ld = pair("wu_ld"), pair("wg_ld"), pair("wdt_ld"), pair("uy_ld")
        bc_ld = [sem(f"bc_ld{g}") for g in range(4)]
        u_st, y_st = sem("u_st"), sem("y_st")
        names = ("setup ln_bn ln_stat ln_sqrt ln_rstd ln_xn ln_tr ln_cp u_mm u_raw u_tap u_conv u_act wx_mm "
                 "rms_dve rms_sqrt ssm_tr ssm_cp dl_mm dl_act dl_add du_ok g_mm g_act "
                 "exp_ok drive_ok scan_ok prod_ok sum_ok y_half y_ok").split()
        counters = [sem(n) for n in names]
        (setup, ln_bn, ln_stat, ln_sqrt, ln_rstd, ln_xn, ln_tr, ln_cp, u_mm, u_raw, u_tap, u_conv, u_act, wx_mm,
         rms_dve, rms_sqrt, ssm_tr, ssm_cp, dl_mm, dl_act, dl_add, du_ok, g_mm, g_act,
         exp_ok, drive_ok, scan_ok, prod_ok, sum_ok, y_half, y_ok) = counters

        with nc.Block() as credits:
            @credits.gpsimd
            def _(pool):
                for s in counters:
                    pool.sem_inc(s, CREDIT)
                for s in (u_st, y_st):
                    pool.sem_inc(s, DMA)

        block = ctx.enter_context(nc.Block())
        v2 = lambda t: t.rearrange("p (x t) -> p x t", x=2)
        hv = lambda t: t[:, :, 0:HALF]
        half = lambda x: slice(HALF * x, HALF * x + HALF)
        RMS_STEPS = 11

        @block.sync
        def _(sp):
            for dst, src in ((w_x[:], a["w_x"]), (a_par[:], a["A"]), (conv_w[:], a["conv_w"]),
                             (conv_b, a["conv_b"]), (dt_bias, a["dt_bias"]), (d_par, a["D"]),
                             (ident[:], a["ident"])):
                sp.dma_start(dst, src).then_inc(cst_ld, DMA)
            for x, name in enumerate(("dt_ln", "b_ln", "c_ln")):
                lo, hi = (0, R, R + N, RBC)[x:x + 2]
                sp.dma_start(ln_w[:, lo:hi], a[name].partition_broadcast(P)).then_inc(cst_ld, DMA)

            def load_h(b):
                for t in range(TT):
                    sp.wait_ge(ln_tr, done(TT * b + t))
                    sp.dma_start(h_t[:], a["h_all"][b, P * t:P * t + P, :]).then_inc(ht_ld, DMA)

            def load_wu(c, place, j):
                sp.wait_ge(u_mm, done(j - 1))
                sp.dma_start(w_u[:, place], row(a["w_u"], c)).then_inc(wu_ld[place], DMA)

            def load_slot(c, place, i):
                sp.wait_ge(dl_mm, done(i - 1))
                sp.dma_start(w_dt[:, place], row(a["w_dt"], c)).then_inc(wdt_ld[place], DMA)
                sp.wait_ge(g_mm, done(i - 1))
                sp.dma_start(w_g[:, place], row(a["w_g"], c)).then_inc(wg_ld[place], DMA)
                sp.wait_ge(y_st, stored(i - 1))
                sp.dma_start(u_y[:, place], row(a["u_scr"], i)).then_inc(uy_ld[place], DMA)

            def store_u(j):
                sp.wait_ge(u_act, done(j + 1))
                sp.dma_start(row(a["u_scr"], j), u_new[:]).then_inc(u_st, DMA)

            def store_y(b, c, place, i):
                sp.wait_ge(y_ok, done(i + 1))
                dst = a["y_scr"][TT * b:TT * b + TT, :, bass.ds(c, 1), :].squeeze(2).rearrange("t p k -> p t k")
                sp.dma_start(dst, u_y[:, place].rearrange("p (t k) -> p t k", t=TT)).then_inc(y_st, DMA)

            def broadcast_bc(b):
                sp.wait_ge(ssm_cp, done(2 * (b + 1)))
                sp.dma_start(a["bc_scr"][b], ssmT[R:RBC, :]).then_inc(bc_st, DMA)
                sp.wait_ge(bc_st, DMA * (b + 1))
                for g in range(4):
                    lo, hi = 4 * g, 4 * g + 4
                    k = N * (DC * b - 1) + hi
                    if b:
                        sp.wait_ge(drive_ok, done(k))
                        sp.wait_ge(prod_ok, done(k))
                    sp.dma_start(b_bc[:, lo:hi, :], a["bc_scr"][b, lo:hi, :].partition_broadcast(P)).then_inc(bc_ld[g], DMA)
                    sp.dma_start(c_bc[:, lo:hi, :],
                                 a["bc_scr"][b, N + lo:N + hi, :].partition_broadcast(P)).then_inc(bc_ld[g], DMA)

            load_h(0)

            with sp.Fori(0, DC // 2) as c2:
                for place in range(2):
                    c = 2 * c2 + place
                    load_wu(c, place, c)
                    store_u(c)
            for b in range(B):
                broadcast_bc(b)
                sp.wait_ge(u_st, stored(DC * (b + 1)))
                load_slot(0, 0, DC * b)
                ahead = b + 1 < B
                if ahead:
                    load_h(b + 1)
                    load_wu(0, 0, DC * (b + 1))

                def slot(c, place, c2, last, b=b, ahead=ahead):
                    i = c + DC * b
                    if not last:
                        load_slot(c + 1, 1 - place, i + 1)
                        if ahead:
                            load_wu(c + 1, 1 - place, i + DC + 1)
                    if ahead:
                        store_u(i + DC)
                    store_y(b, c, place, i)
                over_chunks(sp, slot)
            sp.wait_ge(y_st, stored(DC * B))

        @block.scalar
        def _(act):
            def layer_norm(b):
                for t in range(TT):
                    k = TT * b + t
                    act.wait_ge(ln_stat, done(k + 1))
                    act.activation(mv[:, 2:3], mv[:, 1:2], ACT.Sqrt, bias=consts[:, 0:1]).then_inc(ln_sqrt, 1)
                    act.wait_ge(ln_tr, done(k + 1))
                    if t == 0 and b > 1:
                        act.wait_ge(g_mm, done(DC * (b - 1)))
                    act.copy(xnT[:, b % 2, :, P * t:P * t + P],
                             g0[:].rearrange("p x (k t) -> p (x k) t", t=P)).then_inc(ln_cp, 1)

            def u_out(c, j):
                act.wait_ge(u_mm, done(j + 1))
                act.wait_ge(u_conv, done(3 * j))
                act.copy(v2(raw[:, TAPS - 1:]), hv(g0)).then_inc(u_raw, 1)
                act.wait_ge(wx_mm, done(j))
                act.wait_ge(u_st, stored(j))
                act.activation(v2(u_new[:]), hv(g0), ACT.Identity, bias=conv_b[:, bass.ds(c, 1)],
                               scale=conv_w[:, bass.ds(c * TAPS + TAPS - 1, 1)]).then_inc(u_tap, 1)

            def u_silu(j):
                act.wait_ge(u_conv, done(3 * j + 3))
                act.activation(u_new[:], u_new[:], ACT.Silu).then_inc(u_act, 1)

            def softplus(step, c, place, i):
                bias = dt_bias[:, bass.ds(c, 1)]
                if step == 0:
                    act.wait_ge(dl_mm, done(i + 1))
                    act.wait_ge(du_ok, done(i - 1))
                    act.wait_ge(dl_add, done(i))
                    act.activation(v2(delta[:, place]), hv(g0), ACT.Relu, bias=bias).then_inc(dl_act, 1)
                    act.activation(v2(sp_tmp[:]), hv(g0), ACT.Abs, bias=bias).then_inc(dl_act, 1)
                elif step == 1:
                    act.wait_ge(dl_act, done(4 * i + 2))
                    act.activation(sp_tmp[:], sp_tmp[:], ACT.Exp, scale=-1.0).then_inc(dl_act, 1)
                else:
                    act.wait_ge(dl_act, done(4 * i + 3))
                    act.activation(sp_tmp[:], sp_tmp[:], ACT.Ln, bias=consts[:, 2:3]).then_inc(dl_act, 1)

            def gate(i):
                act.wait_ge(g_mm, done(i + 1))
                act.wait_ge(y_ok, done(i))
                act.activation(v2(s_gate[:]), hv(g1), ACT.Silu).then_inc(g_act, 1)

            def ssm_finish(b):
                act.wait_ge(rms_dve, done(RMS_STEPS * b + 6))
                act.activation(ssm_ms[:], ssm_ms[:], ACT.Sqrt, bias=consts[:, 1:2]).then_inc(rms_sqrt, 1)
                act.wait_ge(ssm_tr, done(b + 1))
                act.copy(ssmT[:, 0:4 * P], g0[0:RBC, 0, :]).then_inc(ssm_cp, 1)
                act.copy(ssmT[:, 4 * P:], g0[0:RBC, 1, 0:P]).then_inc(ssm_cp, 1)

            act.wait_ge(setup, done(3))
            act.wait_ge(cst_ld, DMA * 10)
            layer_norm(0)
            with act.Fori(0, DC // 2) as c2:
                for place in range(2):
                    c = 2 * c2 + place
                    u_out(c, c)
                    u_silu(c)
            for b in range(B):
                ahead = b + 1 < B
                ssm_finish(b)
                for step in range(3):
                    softplus(step, 0, 0, DC * b)
                if ahead:
                    layer_norm(b + 1)

                def slot(c, place, c2, last, b=b, ahead=ahead):
                    i = c + DC * b
                    for n in range(N):
                        k = N * i + n
                        if n == 0:
                            act.wait_ge(dl_add, done(i + 1))
                        act.wait_ge(scan_ok, done(k - RING_A + 1))
                        act.activation(decay[:, n % RING_A], delta[:, place], ACT.Exp,
                                       scale=a_par[:, bass.ds(c * N + n, 1)]).then_inc(exp_ok, 1)
                        if n == 9 and ahead:
                            u_out(c, i + DC)
                        if n >= 13 and not last:
                            softplus(n - 13, c + 1, 1 - place, i + 1)
                    if ahead:
                        u_silu(i + DC)
                    gate(i)
                over_chunks(act, slot)

        @block.gpsimd
        def _(pool):
            for b in range(B):
                def slot(c, place, c2, last, b=b):
                    i = c + DC * b
                    for n in range(N):
                        k = N * i + n
                        if n == 0:
                            pool.wait_ge(du_ok, done(i + 1))
                        if n % 4 == 0:
                            pool.wait_ge(bc_ld[n // 4], 2 * DMA * (b + 1))
                        pool.wait_ge(scan_ok, done(k - RING_U + 1))
                        pool.tensor_tensor(drive[:, n % RING_U], du[:, place], b_bc[:, n], ALU.mult).then_inc(drive_ok, 1)
                over_chunks(pool, slot)

        @block.vector
        def _(dve):
            def layer_norm(b):
                for t in range(TT):
                    k = TT * b + t
                    dve.wait_ge(ht_ld, DMA * (k + 1))
                    for x in range(2):
                        dve.bn_stats(stats[:, x], h_t[:, 512 * x:512 * x + 512]).then_inc(ln_bn, 1)
                    dve.wait_ge(ln_bn, done(2 * k + 2))
                    dve.bn_aggr(mv[:, 0:2], stats[:].rearrange("p x s -> p (x s)")).then_inc(ln_stat, 1)
                    dve.wait_ge(ln_sqrt, done(k + 1))
                    dve.reciprocal(mv[:, 3:4], mv[:, 2:3]).then_inc(ln_rstd, 1)
                    dve.wait_ge(ln_rstd, done(k + 1))
                    dve.tensor_scalar(h_t[:], h_t[:], mv[:, 0:1], mv[:, 3:4], ALU.subtract, ALU.mult).then_inc(ln_xn, 1)

            def conv(s, c, j):
                if s == 0:
                    dve.wait_ge(u_raw, done(j + 1))
                    dve.wait_ge(u_tap, done(j + 1))
                else:
                    dve.wait_ge(u_conv, done(3 * j + s))
                lo = TAPS - 2 - s
                dve.scalar_tensor_tensor(out=u_new[:], in0=raw[:, lo:lo + TOK],
                                         scalar=conv_w[:, bass.ds(c * TAPS + TAPS - 2 - s, 1)], in1=u_new[:],
                                         op0=ALU.mult, op1=ALU.add).then_inc(u_conv, 1)

            def step_size(place, i, uses):
                dve.wait_ge(dl_act, done(4 * i + 4))
                dve.tensor_tensor(delta[:, place], delta[:, place], sp_tmp[:], ALU.add).then_inc(dl_add, 1)
                dve.wait_ge(dl_add, done(i + 1))
                dve.wait_ge(uy_ld[place], DMA * uses)
                dve.tensor_tensor(du[:, place], delta[:, place], u_y[:, place], ALU.mult).then_inc(du_ok, 1)

            def ssm_finish(b):
                at = RMS_STEPS * b
                dve.wait_ge(wx_mm, done(DC * (b + 1)))
                dve.tensor_copy(ssm[:].rearrange("p t r -> p (t r)"), ssm_ps[:, 0:TT * RBC]).then_inc(rms_dve, 1)
                dve.wait_ge(rms_dve, done(at + 1))
                dve.wait_ge(ln_tr, done(TT * (b + 1)))
                sq = h_t[:, 0:TT * RBC].rearrange("p (t r) -> p t r", r=RBC)
                dve.tensor_tensor(sq, ssm[:], ssm[:], ALU.mult).then_inc(rms_dve, 1)
                dve.wait_ge(rms_dve, done(at + 2))
                parts = ((0, R), (R, R + N), (R + N, RBC))
                for x, (lo, hi) in enumerate(parts):
                    dve.tensor_reduce(ssm_ms[:, x], sq[:, :, lo:hi], AX, ALU.add).then_inc(rms_dve, 1)
                dve.wait_ge(rms_dve, done(at + 5))
                dve.tensor_tensor(ssm_ms[:], ssm_ms[:], inv_count[:], ALU.mult).then_inc(rms_dve, 1)
                dve.wait_ge(rms_sqrt, done(b + 1))
                dve.reciprocal(ssm_ms[:], ssm_ms[:]).then_inc(rms_dve, 1)
                dve.wait_ge(rms_dve, done(at + 7))
                for x, (lo, hi) in enumerate(parts):
                    dve.tensor_tensor(ssm[:, :, lo:hi], ssm[:, :, lo:hi],
                                      ssm_ms[:, x].unsqueeze(2).broadcast_to([P, TT, hi - lo]), ALU.mult).then_inc(rms_dve, 1)
                dve.wait_ge(rms_dve, done(at + 10))
                dve.tensor_tensor(ssm[:], ssm[:], ln_w[:].unsqueeze(1).broadcast_to([P, TT, RBC]), ALU.mult).then_inc(rms_dve, 1)

            dve.memset(consts[:, 0:1], LN_EPS).then_inc(setup, 1)
            dve.memset(consts[:, 1:2], RMS_EPS).then_inc(setup, 1)
            dve.memset(consts[:, 2:3], 1.0).then_inc(setup, 1)
            dve.memset(inv_count[:, 0], 1.0 / R).then_inc(setup, 1)
            dve.memset(inv_count[:, 1:3], 1.0 / N).then_inc(setup, 1)
            dve.memset(zero[:], 0.0).then_inc(setup, 1)
            dve.memset(raw[:, 0:TAPS - 1], 0.0).then_inc(setup, 1)
            dve.wait_ge(cst_ld, DMA * 10)
            dve.wait_ge(setup, done(7))
            layer_norm(0)
            with dve.Fori(0, DC // 2) as c2:
                for place in range(2):
                    for s in range(TAPS - 1):
                        conv(s, 2 * c2 + place, 2 * c2 + place)
            for b in range(B):
                ahead = b + 1 < B
                ssm_finish(b)
                step_size(0, DC * b, DC // 2 * b + 1)
                if ahead:
                    layer_norm(b + 1)

                def slot(c, place, c2, last, b=b, ahead=ahead):
                    i = c + DC * b

                    def product(n):
                        k = N * i + n
                        dve.wait_ge(scan_ok, done(k + 1))
                        dve.wait_ge(sum_ok, done(k - RING_C + 1))
                        dve.tensor_tensor(prod[:, n % RING_C], state[:, n % RING_H], c_bc[:, n], ALU.mult).then_inc(prod_ok, 1)

                    for n in range(N):
                        k = N * i + n
                        if n in (8, 9, 10) and ahead:
                            conv(n - 8, c, i + DC)
                        if n % 4 == 0:
                            dve.wait_ge(bc_ld[n // 4], 2 * DMA * (b + 1))
                        dve.wait_ge(exp_ok, done(k + 1))
                        dve.wait_ge(drive_ok, done(k + 1))
                        dve.wait_ge(prod_ok, done(k - RING_H + 1))
                        dve.tensor_tensor_scan(state[:, n % RING_H], decay[:, n % RING_A], drive[:, n % RING_U], 0.0,
                                               ALU.mult, ALU.add).then_inc(scan_ok, 1)
                        if n:
                            product(n - 1)
                    product(N - 1)
                    if not last:
                        step_size(1 - place, i + 1, (DC // 2 * b + 1 + c2) if place == 0 else (DC // 2 * b + 2 + c2))
                    dve.wait_ge(sum_ok, done(N * i + N))
                    dve.scalar_tensor_tensor(out=v2(u_y[:, place]), in0=v2(u_y[:, place]), scalar=d_par[:, bass.ds(c, 1)],
                                             in1=hv(y_ps), op0=ALU.mult, op1=ALU.add).then_inc(y_half, 1)
                    dve.wait_ge(y_half, done(i + 1))
                    dve.wait_ge(g_act, done(i + 1))
                    dve.tensor_tensor(u_y[:, place], u_y[:, place], s_gate[:], ALU.mult).then_inc(y_ok, 1)
                over_chunks(dve, slot)

        @block.tensor
        def _(pe):
            def layer_norm(b):
                for t in range(TT):
                    k = TT * b + t
                    pe.wait_ge(ln_xn, done(k + 1))
                    pe.wait_ge(ln_cp, done(k))
                    if t == 0 and b:
                        pe.wait_ge(dl_act, done(4 * DC * (b - 1) + 4))
                    for m in range(KC):
                        last = pe.transpose(g0[:, m // 4, P * (m % 4):P * (m % 4) + P], h_t[:, P * m:P * m + P], ident[:])
                    last.then_inc(ln_tr, 1)

            def u_step(m, c, place, j, xn):
                for x in range(2):
                    last = pe.matmul(g0[:, x, 0:HALF], w_u[:, place, m, :], xnT[:, xn, m, half(x)],
                                     start=(m == 0), stop=(m == KC - 1))
                if m == KC - 1:
                    last.then_inc(u_mm, 1)

            def clear_ssm():
                pe.matmul(ssm_ps[:, 0:TT * RBC], zero[0:1, 0:P], zero[:], start=True, stop=False, skip_group_check=True)

            def wx(c, j):
                pe.wait_ge(u_act, done(j + 1))
                for t in range(TT):
                    last = pe.matmul(ssm_ps[:, RBC * t:RBC * t + RBC], u_new[:, P * t:P * t + P], w_x[:, bass.ds(c * RBC, RBC)],
                                     start=False, stop=False, skip_group_check=True)
                last.then_inc(wx_mm, 1)

            def ssm_finish(b):
                pe.wait_ge(rms_dve, done(RMS_STEPS * (b + 1)))
                pe.wait_ge(u_tap, done(DC * (b + 1)))
                for t in range(TT):
                    last = pe.transpose(g0[0:RBC, t // 4, P * (t % 4):P * (t % 4) + P], ssm[:, t, :], ident[:])
                last.then_inc(ssm_tr, 1)

            def step_product(place, i, uses):
                pe.wait_ge(wdt_ld[place], DMA * uses)
                for x in range(2):
                    last = pe.matmul(g0[:, x, 0:HALF], w_dt[:, place, :], ssmT[0:R, half(x)], start=True, stop=True)
                last.then_inc(dl_mm, 1)

            pe.wait_ge(cst_ld, DMA * 10)
            pe.wait_ge(setup, done(7))
            layer_norm(0)
            clear_ssm()
            pe.wait_ge(ln_cp, done(TT))
            with pe.Fori(0, DC // 2) as c2:
                for place in range(2):
                    c = 2 * c2 + place
                    pe.wait_ge(wu_ld[place], DMA * (c2 + 1))
                    pe.wait_ge(u_tap, done(c))
                    for m in range(KC):
                        u_step(m, c, place, c, 0)
                    wx(c, c)
            for b in range(B):
                ahead = b + 1 < B
                ssm_finish(b)
                pe.wait_ge(ssm_cp, done(2 * (b + 1)))
                step_product(0, DC * b, DC // 2 * b + 1)
                if ahead:
                    layer_norm(b + 1)
                    clear_ssm()
                    pe.wait_ge(ln_cp, done(TT * (b + 2)))

                def slot(c, place, c2, last, b=b, ahead=ahead):
                    i = c + DC * b
                    j = i + DC
                    for n in range(N):
                        k = N * i + n
                        if n == 0 and ahead:
                            pe.wait_ge(wu_ld[place], DMA * (DC // 2 * (b + 1) + c2 + 1))
                            pe.wait_ge(dl_act, done(4 * i + 4))
                        if n < 4 and ahead:
                            u_step(2 * n, c, place, j, (b + 1) % 2)
                            u_step(2 * n + 1, c, place, j, (b + 1) % 2)
                        if n == 4:
                            pe.wait_ge(wg_ld[place], DMA * (DC // 2 * b + c2 + 1))
                            pe.wait_ge(g_act, done(i))
                        if 4 <= n < 4 + KC:
                            m = n - 4
                            for x in range(2):
                                mm = pe.matmul(g1[:, x, 0:HALF], w_g[:, place, m, :], xnT[:, b % 2, m, half(x)],
                                               start=(m == 0), stop=(m == KC - 1))
                            if m == KC - 1:
                                mm.then_inc(g_mm, 1)
                        if n == 9 and not last:
                            if ahead:
                                pe.wait_ge(u_tap, done(j + 1))
                            else:
                                pe.wait_ge(dl_act, done(4 * i + 4))
                            step_product(1 - place, i + 1, (DC // 2 * b + 1 + c2) if place == 0 else (DC // 2 * b + 2 + c2))
                        if n == 0:
                            pe.wait_ge(y_half, done(i))
                        pe.wait_ge(prod_ok, done(k + 1))
                        for x in range(2):
                            mm = pe.matmul(y_ps[:, x, 0:HALF], ident[:], prod[:, n % RING_C, half(x)],
                                           start=(n == 0), stop=(n == N - 1))
                        mm.then_inc(sum_ok, 1)
                    if ahead:
                        wx(c, j)
                over_chunks(pe, slot)


def output_part(nc, a, sem):
    TILES = B * TT
    with ExitStack() as ctx:
        sb = lambda name, shape: ctx.enter_context(nc.sbuf_tensor(name, shape, F32))
        pair = lambda name: [sem(f"{name}{x}") for x in range(2)]
        w_out, w_a, w_b = sb("w_out_sb", [P, DC, L]), sb("w_a_sb", [P, KC, BN]), sb("w_b_sb", [P, MC, L])
        w_q, keys = sb("w_q_sb", [P, KC, RD]), sb("keys_sb", [RD, E])
        ident = sb("o_ident", [P, P])
        y_t = sb("y_t", [P, 2, DC, P])
        h = sb("o_h", [P, 2, L])
        xn = sb("o_xn", [P, L])
        xnT = sb("o_xnT", [P, KC, P])
        zg, zgT = sb("zg", [P, BN]), sb("zgT", [P, MC, P])
        qT = sb("qT", [RD, P])
        score, left, ex = sb("score", [P, E]), sb("left", [P, 2, E]), sb("ex", [P, E])
        top = sb("top", [P, 2, 8])
        carrier = sb("carrier", [P, 5])
        scal = sb("scal", [P, 4])
        stats, mv, eps = sb("o_stats", [P, 2, 6]), sb("o_mv", [P, 4]), sb("o_eps", [P, 1])
        psum = lambda name, shape: ctx.enter_context(nc.psum_tensor(name, shape, F32))
        o_ps, t_ps, f_ps = psum("o_ps", [P, L]), psum("t_ps", [P, L]), psum("f_ps", [P, L])
        z_ps, s_ps = psum("z_ps", [P, BN]), psum("s_ps", [P, 512])

        ld, y_ld, h_ld, out_st = sem("o_ld"), pair("y_ld"), pair("h_ld"), pair("out_st")
        names = ("o_setup o_mm h2_half h2_ok o_bn o_stat o_sqrt o_rstd xn_ok xt_mm xt_cp q_mm q_cp z_mm s_mm "
                 "carried sel sel_r sel_exp zg_ok zt_mm zt_cp f_mm out_ok").split()
        counters = [sem(n) for n in names]
        (o_setup, o_mm, h2_half, h2_ok, o_bn, o_stat, o_sqrt, o_rstd, xn_ok, xt_mm, xt_cp, q_mm, q_cp, z_mm, s_mm,
         carried, sel, sel_r, sel_exp, zg_ok, zt_mm, zt_cp, f_mm, out_ok) = counters
        with nc.Block() as credits:
            @credits.gpsimd
            def _(pool):
                for s in counters:
                    pool.sem_inc(s, CREDIT)
                for s in out_st:
                    pool.sem_inc(s, DMA)
        block = ctx.enter_context(nc.Block())
        SEL = 9

        def over_tiles(eng, body):
            with eng.Fori(0, TILES // 2 - 1) as q2:
                for place in range(2):
                    body(2 * q2 + place, place, q2, False)
            for place in range(2):
                body(TILES - 2 + place, place, TILES // 2 - 1, place == 1)

        @block.sync
        def _(sp):
            for dst, src in ((w_out[:], a["w_out"]), (w_a[:], a["w_a"]), (w_b[:], a["w_b"]),
                             (w_q[:], a["w_q"]), (keys[:], a["keysT"]), (ident[:], a["ident"])):
                sp.dma_start(dst, src).then_inc(ld, DMA)

            def load(q, place):
                sp.wait_ge(o_mm, done(q - 1))
                sp.dma_start(y_t[:, place], row(a["y_scr"], q)).then_inc(y_ld[place], DMA)

            def load_h(q, place, uses):
                sp.wait_ge(out_st[place], stored(uses))
                sp.dma_start(h[:, place], row(a["h_rows"], q)).then_inc(h_ld[place], DMA)

            load(0, 0)
            load_h(0, 0, 0)

            def tile(q, place, q2, last):
                if not last:
                    load(q + 1, 1 - place)
                    load_h(q + 1, 1 - place, q2 if place == 0 else q2 + 1)
                sp.wait_ge(out_ok, done(q + 1))
                sp.dma_start(row(a["out"], q), h[:, place]).then_inc(out_st[place], DMA)
            over_tiles(sp, tile)
            for s in out_st:
                sp.wait_ge(s, stored(TILES // 2))

        @block.tensor
        def _(pe):
            def project(q, place, uses):
                pe.wait_ge(y_ld[place], DMA * uses)
                pe.wait_ge(h2_ok, done(q))
                for c in range(DC):
                    for x in range(2):
                        last = pe.matmul(o_ps[:, 512 * x:512 * x + 512], y_t[:, place, c, :], w_out[:, c, 512 * x:512 * x + 512],
                                         start=(c == 0), stop=(c == DC - 1))
                last.then_inc(o_mm, 1)

            pe.wait_ge(ld, DMA * 6)
            project(0, 0, 1)

            def tile(q, place, q2, last):
                pe.wait_ge(xn_ok, done(q + 1))
                pe.wait_ge(zt_cp, done(q))
                for m in range(KC):
                    mm = pe.transpose(t_ps[:, P * m:P * m + P], xn[:, P * m:P * m + P], ident[:])
                mm.then_inc(xt_mm, 1)
                pe.wait_ge(xt_cp, done(q + 1))
                for m in range(KC):
                    mm = pe.matmul(s_ps[0:RD, 0:P], w_q[:, m, :], xnT[:, m, :], start=(m == 0), stop=(m == KC - 1))
                mm.then_inc(q_mm, 1)
                pe.wait_ge(zg_ok, done(q))
                for m in range(KC):
                    mm = pe.matmul(z_ps[:], xnT[:, m, :], w_a[:, m, :], start=(m == 0), stop=(m == KC - 1))
                mm.then_inc(z_mm, 1)
                pe.wait_ge(q_cp, done(q + 1))
                pe.matmul(s_ps[:, P:P + E], qT[:], keys[:], start=True, stop=True).then_inc(s_mm, 1)
                if not last:
                    project(q + 1, 1 - place, (q2 + 1) if place == 0 else (q2 + 2))
                pe.wait_ge(zg_ok, done(q + 1))
                for m in range(MC):
                    mm = pe.transpose(t_ps[:, P * m:P * m + P], zg[:, P * m:P * m + P], ident[:])
                mm.then_inc(zt_mm, 1)
                pe.wait_ge(zt_cp, done(q + 1))
                pe.wait_ge(out_ok, done(q))
                for m in range(MC):
                    for x in range(2):
                        mm = pe.matmul(f_ps[:, 512 * x:512 * x + 512], zgT[:, m, :], w_b[:, m, 512 * x:512 * x + 512],
                                       start=(m == 0), stop=(m == MC - 1))
                mm.then_inc(f_mm, 1)
            over_tiles(pe, tile)

        @block.scalar
        def _(act):
            def deviation(q):
                act.wait_ge(o_stat, done(q + 1))
                act.activation(mv[:, 2:3], mv[:, 1:2], ACT.Sqrt, bias=eps[:]).then_inc(o_sqrt, 1)

            act.wait_ge(o_setup, done(1))
            deviation(0)

            def tile(q, place, q2, last):
                act.wait_ge(xt_mm, done(q + 1))
                act.wait_ge(z_mm, done(q))
                act.copy(xnT[:].rearrange("p k t -> p (k t)"), t_ps[:]).then_inc(xt_cp, 1)
                act.wait_ge(q_mm, done(q + 1))
                act.copy(qT[:], s_ps[0:RD, 0:P]).then_inc(q_cp, 1)
                act.wait_ge(sel, done(SEL * q + 3))
                act.activation(ex[:], score[:], ACT.Exp, bias=scal[:, 0:1]).then_inc(sel_exp, 1)
                if not last:
                    deviation(q + 1)
                act.wait_ge(zt_mm, done(q + 1))
                act.wait_ge(f_mm, done(q))
                act.copy(zgT[:].rearrange("p m t -> p (m t)"), t_ps[:, 0:BN]).then_inc(zt_cp, 1)
            over_tiles(act, tile)

        @block.vector
        def _(dve):
            def front(q, place, uses):
                dve.wait_ge(o_mm, done(q + 1))
                dve.wait_ge(h_ld[place], DMA * uses)
                dve.tensor_tensor(h[:, place], h[:, place], o_ps[:], ALU.add).then_inc(h2_ok, 1)
                dve.wait_ge(h2_ok, done(q + 1))
                for x in range(2):
                    dve.bn_stats(stats[:, x], h[:, place, 512 * x:512 * x + 512]).then_inc(o_bn, 1)
                dve.wait_ge(o_bn, done(2 * q + 2))
                dve.tensor_copy(carrier[:, 0:1], stats[:, 0, 0:1]).then_inc(carried, 1)
                dve.bn_aggr(mv[:, 0:2], stats[:].rearrange("p x s -> p (x s)")).then_inc(o_stat, 1)
                dve.wait_ge(o_sqrt, done(q + 1))
                dve.reciprocal(mv[:, 3:4], mv[:, 2:3]).then_inc(o_rstd, 1)
                dve.wait_ge(o_rstd, done(q + 1))
                dve.wait_ge(xt_mm, done(q))
                dve.tensor_scalar(xn[:], h[:, place], mv[:, 0:1], mv[:, 3:4], ALU.subtract, ALU.mult).then_inc(xn_ok, 1)

            dve.memset(eps[:], LN_EPS).then_inc(o_setup, 1)
            front(0, 0, 1)

            def tile(q, place, q2, last):
                at = q * SEL

                def link(step, ins):
                    ins.then_inc(sel, 1)
                    dve.wait_ge(sel, done(at + step))

                dve.wait_ge(s_mm, done(q + 1))
                link(1, dve.tensor_copy(score[:], s_ps[:, P:P + E]))
                dve.tensor_copy(carrier[:, 1:2], score[:, 0:1]).then_inc(carried, 1)
                link(2, dve.max(top[:, 0], score[:]))
                link(3, dve.tensor_scalar(scal[:, 0:1], top[:, 0, 0:1], -1.0, None, ALU.mult))
                dve.tensor_copy(carrier[:, 2:3], scal[:, 0:1]).then_inc(carried, 1)
                link(4, dve.match_replace(left[:, 0], top[:, 0], score[:], -3.0e38))
                dve.tensor_copy(carrier[:, 3:4], left[:, 0, 0:1]).then_inc(carried, 1)
                link(5, dve.max(top[:, 1], left[:, 0]))
                dve.tensor_copy(carrier[:, 4:5], top[:, 1, 0:1]).then_inc(carried, 1)
                link(6, dve.match_replace(left[:, 1], top[:, 1], left[:, 0], -3.0e38))
                link(7, dve.tensor_tensor(left[:, 0], score[:], left[:, 1], ALU.not_equal))
                dve.wait_ge(sel_exp, done(q + 1))
                link(8, dve.tensor_tensor(ex[:], ex[:], left[:, 0], ALU.mult))
                dve.tensor_reduce(scal[:, 1:2], ex[:], AX, ALU.add).then_inc(sel, 1)
                dve.wait_ge(sel, done(at + 9))
                dve.reciprocal(scal[:, 2:3], scal[:, 1:2]).then_inc(sel_r, 1)
                dve.wait_ge(sel_r, done(2 * q + 1))
                dve.tensor_scalar(ex[:], ex[:], scal[:, 2:3], 2.0, ALU.mult, ALU.mult).then_inc(sel_r, 1)
                dve.wait_ge(sel_r, done(2 * q + 2))
                dve.wait_ge(z_mm, done(q + 1))
                dve.wait_ge(zt_mm, done(q))
                dve.tensor_tensor(zg[:].rearrange("p (e r) -> p e r", e=E), z_ps[:].rearrange("p (e r) -> p e r", e=E),
                                  ex[:].unsqueeze(2).broadcast_to([P, E, RANK]), ALU.mult).then_inc(zg_ok, 1)
                if not last:
                    front(q + 1, 1 - place, (q2 + 1) if place == 0 else (q2 + 2))
                dve.wait_ge(f_mm, done(q + 1))
                dve.tensor_tensor(h[:, place], h[:, place], f_ps[:], ALU.add).then_inc(out_ok, 1)
            over_tiles(dve, tile)


def build(nc, a):
    with ExitStack() as ctx:
        sem = lambda name: ctx.enter_context(nc.semaphore(name))
        tokens_part(nc, a, sem)
        mixer_part(nc, a, sem)
        output_part(nc, a, sem)


def constants():
    t = np.zeros((P, NV + 8), np.float32)
    t[:, 0:NA] = 64 * np.arange(NA)
    t[:, NA:NA + NB1] = NB2 * np.arange(NB1)
    t[:, NA + NB1:NV] = np.arange(NB2)
    re = np.arange(P) < 64
    t[:, NV] = np.where(re, 0.25, 0)
    t[:, NV + 1] = np.where(re, 0, 0.25)
    t[:, NV + 2] = np.where(re, np.pi / 2, 0)
    t[:, NV + 3] = np.where(re, 0, np.pi / 2)
    t[:, NV + 4] = np.where(re, 1, -1)
    t[:, NV + 5] = -t[:, NV + 4]
    return t


def layouts(x):
    cont = np.ascontiguousarray
    per_chunk = lambda v, w: cont(v.reshape(DC, P, w).transpose(1, 0, 2).reshape(P, DC * w))
    lhs = lambda w: cont(w.reshape(DC, P, KC, P).transpose(0, 3, 2, 1))
    rhs = lambda w, k: cont(w.T.reshape(k, P, w.shape[0]).transpose(1, 0, 2))
    s4, w_in = x["x"], x["L0_attn_W_in"]
    return {
        "aimT": cont(x["L0_tok_A_imag"].T), "iarT": cont(x["L0_tok_inv_A_real"].T),
        "brT": cont(x["L0_tok_B"][..., 0].T), "biT": cont(x["L0_tok_B"][..., 1].T),
        "crT": cont(s4[..., 0].transpose(2, 0, 1)), "ciT": cont(s4[..., 1].transpose(2, 0, 1)),
        "log_dt": x["L0_tok_log_dt"], "txt": x["txt"],
        "w_u": lhs(w_in[:D]), "w_g": lhs(w_in[D:]),
        "w_dt": cont(x["L0_attn_Wdt"].reshape(DC, P, R).transpose(0, 2, 1)),
        "w_x": rhs(x["L0_attn_Wx"], DC).reshape(P, DC * RBC),
        "A": per_chunk(x["L0_attn_A"], N), "conv_w": per_chunk(x["L0_attn_conv_w"], TAPS),
        "conv_b": per_chunk(x["L0_attn_conv_b"], 1), "dt_bias": per_chunk(x["L0_attn_dt_bias"], 1),
        "D": per_chunk(x["L0_attn_D_param"], 1),
        "dt_ln": x["L0_attn_dt_ln_w"], "b_ln": x["L0_attn_b_ln_w"], "c_ln": x["L0_attn_c_ln_w"],
        "w_out": rhs(x["L0_attn_W_out"], DC), "w_a": rhs(x["L0_ffn_A_w"], KC), "w_b": rhs(x["L0_ffn_B_w"], MC),
        "w_q": rhs(x["L0_ffn_Wq_w"], KC), "keysT": cont(x["L0_ffn_keys"].T),
        "cst": constants(), "ident": np.eye(P, dtype=np.float32),
    }


def kernel(**inputs):
    import concourse.bacc as bacc
    from concourse.bass_utils import run_bass_kernel_spmd

    nc = bacc.Bacc("TRN2", target_bir_lowering=False, num_devices=1)
    arrays = layouts({k: np.asarray(v) for k, v in inputs.items()})
    a = {k: nc.dram_tensor(f"in_{k}", v.shape, F32, kind="ExternalInput").ap() for k, v in arrays.items()}
    for name, shape in (("h_all", [B, TOK, L]), ("u_scr", [B * DC, P, TOK]), ("y_scr", [B * TT, P, DC, P]),
                        ("bc_scr", [B, 2 * N, TOK])):
        a[name] = nc.dram_tensor(name, shape, F32, kind="Internal").ap()
    out = nc.dram_tensor("out", [B, TOK, L], F32, kind="ExternalOutput").ap()
    tiles = lambda t: t.rearrange("b (t p) l -> (b t) p l", p=P)
    a["h_rows"], a["out"] = tiles(a["h_all"]), tiles(out)
    build(nc, a)
    r = run_bass_kernel_spmd(nc, [{f"in_{k}": v for k, v in arrays.items()}], core_ids=[0])
    return r.results[0]["out"]
```

```python
import numpy as np
from contextlib import ExitStack

import concourse.bass as bass
from concourse import mybir

P = 128
F32 = mybir.dt.float32
ALU = mybir.AluOpType
ACT = mybir.ActivationFunctionType
AX = mybir.AxisListType.X

B = 4
HS, NS = 128, 64
L = 1024
KC = L // P
TOK = 640
TT = TOK // P
HALF = TOK // 2
D = 2048
DC = D // P
N = 16
R = 64
RBC = R + 2 * N
TAPS = 4
E = 64
RANK = 8
RD = 16
BN = E * RANK
MC = BN // P

NA, NB1, NB2 = 16, 8, 8
NV = NA + NB1 + NB2
TWO_PI_HI = 6.28125
TWO_PI_MID = 0.0019350051879882812
TWO_PI_LO = 2 * np.pi - TWO_PI_HI - TWO_PI_MID
ROUND = 1.5 * 2.0 ** 23
PI_MAX = 3.1415925
LN_EPS = 1e-5
RMS_EPS = 1e-6


def tokens_part(nc, a, sem):
    with ExitStack() as ctx:
        sb = lambda name, shape: ctx.enter_context(nc.sbuf_tensor(name, shape, F32))
        cst = sb("t_cst", [P, NV + 8])
        aim, iar, br, bi, ldt = (sb(f"t_{x}", [P, HS]) for x in ("aim", "iar", "br", "bi", "ldt"))
        cr, ci = sb("t_cr", [P, B, HS]), sb("t_ci", [P, B, HS])
        small = {x: sb(f"t_s_{x}", [P, HS]) for x in (
            "are", "dt", "zr", "zi", "den", "rden", "inr", "ini", "nr", "p0", "p1", "mr", "mi", "gr", "gi", "gb", "gbn")}
        two = sb("t_two", [P, 2, HS, NV])
        th, kk = two[:, 0], two[:, 1]
        mag = sb("t_mag", [P, HS, NV])
        own, swp = sb("t_own", [P, HS, NV]), sb("t_swp", [P, HS, NV])
        h_re, h_im, h_sg = (sb(f"t_h{x}", [P, HS, NB2]) for x in ("re", "im", "sg"))
        e2 = sb("t_e2", [P, HS, NB1 * NB2])
        q_own, q_swp, q_tmp = (sb(f"t_q{x}", [P, HS, NA]) for x in ("own", "swp", "tmp"))
        ca, cb = sb("t_ca", [P, HS, B]), sb("t_cb", [P, HS, B])
        w = sb("t_w", [P, HS, B * NA])
        tmp = two[:].rearrange("p x h v -> p (x h v)").rearrange("p (h v) -> p h v", h=HS)
        kout = mag[:].rearrange("p h v -> p (h v)").rearrange("p (h v) -> p h v", h=HS // 2)
        ps = [ctx.enter_context(nc.psum_tensor(f"t_ps{g}", [P, 8, 64], F32)) for g in range(8)]
        ld, dv, ac, mm, ev, st = (sem(f"t_{x}") for x in ("ld", "dv", "ac", "mm", "ev", "st"))
        marks = {}
        block = ctx.enter_context(nc.Block())

        lv = cst[:, 0:NV]
        ph = [cst[:, NV:NV + 1], cst[:, NV + 1:NV + 2]]
        ph2pi = [cst[:, NV + 2:NV + 3], cst[:, NV + 3:NV + 4]]
        sgn, nsgn = cst[:, NV + 4:NV + 5], cst[:, NV + 5:NV + 6]

        def over_v(x, n):
            return x.unsqueeze(2).broadcast_to([P, HS, n])

        @block.sync
        def _(sp):
            n = 0
            for half in range(2):
                rows = slice(64 * half, 64 * half + 64)
                for dst, src in ((aim, a["aimT"]), (iar, a["iarT"]), (br, a["brT"]), (bi, a["biT"])):
                    sp.dma_start(dst[rows, :], src).then_inc(ld, 16)
                sp.dma_start(cr[rows, :, :], a["crT"]).then_inc(ld, 16)
                sp.dma_start(ci[rows, :, :], a["ciT"]).then_inc(ld, 16)
                n += 6
            sp.dma_start(ldt[:, :], a["log_dt"].partition_broadcast(P)).then_inc(ld, 16)
            sp.dma_start(cst[:, :], a["cst"]).then_inc(ld, 16)
            assert n + 2 == 14
            sp.wait_ge(ev, 8)
            for hh in range(2):
                for c in range(B):
                    p0 = 64 * hh + NA * c
                    dst = a["h_all"][c, 64 * hh:64 * hh + 64, :].rearrange("h (a b) -> a h b", a=NA)
                    sp.dma_start(dst, kout[p0:p0 + NA, :, :]).then_inc(st, 16)
            for c in range(B):
                sp.dma_start(a["h_all"][c, P:TOK, :], a["txt"][c]).then_inc(st, 16)
            sp.wait_ge(st, 16 * 12)

        count = [0]
        marks_mag = 4
        marks_arg = (11, 18)

        @block.scalar
        def _(act):
            act.wait_ge(ld, 16 * 14)
            act.activation(small["dt"][:], ldt[:], ACT.Exp).then_inc(ac, 1)
            act.activation(small["are"][:], iar[:], ACT.Exp).then_inc(ac, 1)
            act.wait_ge(dv, marks_mag)
            act.activation(mag[:], mag[:], ACT.Exp).then_inc(ac, 1)
            for x, (t, m) in enumerate(((own, marks_arg[0]), (swp, marks_arg[1]))):
                act.wait_ge(dv, m)
                act.activation(t[:], t[:], ACT.Sin).then_inc(ac, 1)

        @block.vector
        def _(dve):
            def link(ins):
                count[0] += 1
                ins.then_inc(dv, 1)
                dve.wait_ge(dv, count[0])

            s = small
            dve.wait_ge(ac, 2)
            dve.wait_ge(ld, 16 * 14)
            link(dve.scalar_tensor_tensor(out=s["zr"][:], in0=s["are"][:], scalar=-1.0, in1=s["dt"][:],
                                          op0=ALU.mult, op1=ALU.mult))
            link(dve.tensor_tensor(s["zi"][:], aim[:], s["dt"][:], ALU.mult))
            lvb = lv.unsqueeze(1).broadcast_to([P, HS, NV])
            link(dve.tensor_tensor(th, over_v(s["zi"][:], NV), lvb, ALU.mult))
            link(dve.tensor_tensor(mag[:], over_v(s["zr"][:], NV), lvb, ALU.mult))
            assert count[0] == marks_mag
            for x, t in enumerate((own, swp)):
                link(dve.tensor_scalar(kk, th, float(1 / (2 * np.pi)), ph[x], ALU.mult, ALU.add))
                link(dve.tensor_scalar(kk, kk, ROUND, -ROUND, ALU.add, ALU.add))
                link(dve.scalar_tensor_tensor(out=t[:], in0=kk, scalar=-TWO_PI_HI, in1=th, op0=ALU.mult, op1=ALU.add))
                link(dve.scalar_tensor_tensor(out=t[:], in0=kk, scalar=-TWO_PI_MID, in1=t[:], op0=ALU.mult, op1=ALU.add))
                link(dve.scalar_tensor_tensor(out=t[:], in0=kk, scalar=-TWO_PI_LO, in1=t[:], op0=ALU.mult, op1=ALU.add))
                link(dve.tensor_scalar(t[:], t[:], ph2pi[x], PI_MAX, ALU.add, ALU.min))
                link(dve.tensor_scalar(t[:], t[:], -PI_MAX, None, ALU.max))
                assert count[0] == marks_arg[x]
            for x, t in enumerate((own, swp)):
                dve.wait_ge(ac, 4 + x)
                link(dve.tensor_tensor(t[:], t[:], mag[:], ALU.mult))
            lo, hi = slice(0, 64), slice(64, P)
            v2 = slice(NA + NB1, NV)
            for dst, first, second in ((h_re, own, swp), (h_im, swp, own)):
                link(dve.tensor_copy(dst[lo, :, :], first[lo, :, v2]))
                link(dve.tensor_copy(dst[hi, :, :], second[hi, :, v2]))
            link(dve.tensor_scalar(h_sg[:], h_im[:], nsgn, None, ALU.mult))
            shape = [P, HS, NB1, NB2]
            e2v = e2[:].rearrange("p h (x y) -> p h x y", x=NB1)
            tmpv = tmp.rearrange("p h (x y) -> p h x y", x=NB1)
            b1 = slice(NA, NA + NB1)
            link(dve.tensor_tensor(e2v, own[:, :, b1].unsqueeze(3).broadcast_to(shape),
                                   h_re[:].unsqueeze(2).broadcast_to(shape), ALU.mult))
            link(dve.tensor_tensor(tmpv, swp[:, :, b1].unsqueeze(3).broadcast_to(shape),
                                   h_sg[:].unsqueeze(2).broadcast_to(shape), ALU.mult))
            link(dve.tensor_tensor(e2[:], e2[:], tmp, ALU.add))
            tt = lambda o, x, y, op: link(dve.tensor_tensor(s[o][:], x, y, op))
            tt("den", s["are"][:], s["are"][:], ALU.mult)
            tt("p0", aim[:], aim[:], ALU.mult)
            tt("den", s["den"][:], s["p0"][:], ALU.add)
            link(dve.reciprocal(s["rden"][:], s["den"][:]))
            link(dve.scalar_tensor_tensor(out=s["inr"][:], in0=s["are"][:], scalar=-1.0, in1=s["rden"][:],
                                          op0=ALU.mult, op1=ALU.mult))
            link(dve.scalar_tensor_tensor(out=s["ini"][:], in0=aim[:], scalar=-1.0, in1=s["rden"][:],
                                          op0=ALU.mult, op1=ALU.mult))
            link(dve.tensor_scalar(s["nr"][:], h_re[:, :, 1], -1.0, None, ALU.add))
            ni = h_im[:, :, 1]

            def complex_product(ore, oim, xr, xi, yr, yi):
                tt("p0", xr, yr, ALU.mult)
                tt("p1", xi, yi, ALU.mult)
                tt(ore, s["p0"][:], s["p1"][:], ALU.subtract)
                tt("p0", xr, yi, ALU.mult)
                tt("p1", xi, yr, ALU.mult)
                tt(oim, s["p0"][:], s["p1"][:], ALU.add)

            complex_product("mr", "mi", s["nr"][:], ni, s["inr"][:], s["ini"][:])
            complex_product("gr", "gi", br[:], bi[:], s["mr"][:], s["mi"][:])
            link(dve.tensor_scalar(s["gr"][:], s["gr"][:], 2.0, None, ALU.mult))
            link(dve.tensor_scalar(s["gb"][:], s["gi"][:], nsgn, 2.0, ALU.mult, ALU.mult))
            link(dve.tensor_scalar(s["gbn"][:], s["gb"][:], -1.0, None, ALU.mult))
            va = slice(0, NA)
            for dst, first, second, g2 in ((q_own, own, swp, "gb"), (q_swp, swp, own, "gbn")):
                link(dve.tensor_tensor(dst[:], first[:, :, va], over_v(s["gr"][:], NA), ALU.mult))
                link(dve.tensor_tensor(q_tmp[:], second[:, :, va], over_v(s[g2][:], NA), ALU.mult))
                link(dve.tensor_tensor(dst[:], dst[:], q_tmp[:], ALU.add))
            link(dve.tensor_scalar(ca[:].rearrange("p h c -> p c h"), cr[:], sgn, None, ALU.mult))
            link(dve.tensor_scalar(cb[:].rearrange("p h c -> p c h"), ci[:], -1.0, None, ALU.mult))
            shape = [P, HS, B, NA]
            wv = w[:].rearrange("p h (c x) -> p h c x", c=B)
            tmpw = tmp.rearrange("p h (c x) -> p h c x", c=B)
            link(dve.tensor_tensor(wv, q_own[:].unsqueeze(2).broadcast_to(shape),
                                   ca[:].unsqueeze(3).broadcast_to(shape), ALU.mult))
            link(dve.tensor_tensor(tmpw, q_swp[:].unsqueeze(2).broadcast_to(shape),
                                   cb[:].unsqueeze(3).broadcast_to(shape), ALU.mult))
            link(dve.tensor_tensor(w[:], w[:], tmp, ALU.add))
            marks["w"] = count[0]
            for g in range(8):
                dve.wait_ge(mm, g + 1)
                dve.tensor_copy(kout[:, 8 * g:8 * g + 8, :], ps[g][:]).then_inc(ev, 1)

        @block.tensor
        def _(pe):
            pe.wait_ge(dv, marks["w"])
            for g in range(8):
                for x in range(8):
                    for hh in range(2):
                        h = 64 * hh + 8 * g + x
                        last = pe.matmul(ps[g][64 * hh:64 * hh + 64, x, :], w[:, h, :], e2[:, h, :],
                                         start=True, stop=True)
                last.then_inc(mm, 1)


CREDIT = 4
DMA = 16
RING_A, RING_U, RING_C = 4, 2, 2
SHARE = 4


def done(count):
    return count + CREDIT


def stored(count):
    return DMA * count + DMA


def over_chunks(eng, body):
    with eng.Fori(0, DC // 2 - 1) as c2:
        for place in range(2):
            body(2 * c2 + place, place, c2, False)
    for place in range(2):
        body(DC - 2 + place, place, DC // 2 - 1, place == 1)


def row(t, i):
    return t[bass.ds(i, 1)].squeeze(0)


def mixer_part(nc, a, sem):
    with ExitStack() as ctx:
        sb = lambda name, shape: ctx.enter_context(nc.sbuf_tensor(name, shape, F32))
        pair = lambda name: [sem(f"{name}{x}") for x in range(2)]

        b_bc, c_bc = sb("b_bc", [P, N, TOK]), sb("c_bc", [P, N, TOK])
        xnT = sb("xnT", [P, 2, KC, TOK])
        decay = sb("decay", [P, RING_A, TOK])
        drive = sb("drive", [P, RING_U, TOK])
        prod = sb("prod", [P, RING_C, TOK])
        u_new = sb("u_new", [P, TOK])
        raw = sb("raw", [P, TAPS - 1 + TOK])
        u_y = sb("u_y", [P, 2, TOK])
        delta = sb("delta", [P, 2, TOK])
        du = sb("du", [P, 2, TOK])
        s_gate = sb("s_gate", [P, TOK])
        sp_tmp = sb("sp_tmp", [P, TOK])
        ssmT = sb("ssmT", [RBC, TOK])
        w_u = sb("w_u_sb", [P, 2, KC, P])
        w_g = sb("w_g_sb", [P, 2, KC, P])
        w_dt = sb("w_dt_sb", [R, 2, P])
        w_x = sb("w_x_sb", [P, DC * RBC])
        a_par = sb("a_par", [P, DC * N])
        conv_w = sb("conv_w_sb", [P, DC * TAPS])
        vec = sb("vec", [P, 3 * DC])
        conv_b, dt_bias, d_par = (vec[:, DC * x:DC * x + DC] for x in range(3))
        ln_w = sb("ln_w", [P, RBC])
        ident = sb("ident_sb", [P, P])
        h_t = sb("h_t", [P, 2, L])
        stats = sb("stats", [P, 2, 2, 6])
        mv = sb("mv", [P, 4])
        ssm = sb("ssm", [P, TT, RBC])
        ssm_ms = sb("ssm_ms", [P, 3, TT])
        ssm_r = sb("ssm_r", [P, 3, TT])
        ssm_t = sb("ssm_t", [P, 3, TT])
        inv_count = sb("inv_count", [P, 3, TT])
        consts = sb("consts", [P, 3])
        zero = sb("zero", [1, TT * RBC])

        bank_pair = lambda name: ctx.enter_context(nc.psum_tensor(name, [P, 2, 512], F32))
        y_ps, g0, state_ps = bank_pair("y_ps"), bank_pair("g0"), bank_pair("state_ps")
        state = state_ps[:].rearrange("p x t -> p (x t)")[:, 0:TOK]
        g1 = ctx.enter_context(nc.psum_tensor("g1", [P, 512], F32))
        ssm_ps = ctx.enter_context(nc.psum_tensor("ssm_ps", [P, 512], F32))

        cst_ld, ht_ld, bc_st = sem("cst_ld"), pair("ht_ld"), sem("bc_st")
        wu_ld, wg_ld, wdt_ld, uy_ld = pair("wu_ld"), pair("wg_ld"), pair("wdt_ld"), pair("uy_ld")
        bc_ld = [sem(f"bc_ld{g}") for g in range(4)]
        u_st, y_st = sem("u_st"), sem("y_st")
        names = ("setup ln_bn ln_stat ln_root ln_newton ln_xn ln_tr ln_cp u_mm u_raw u_tap u_conv u_act wx_mm "
                 "rms_dve rms_root ssm_tr ssm_cp dl_mm dl_act dl_add du_ok g_mm g_act "
                 "exp_ok drive_ok drive_own scan_ok prod_ok sum_ok y_half y_ok").split()
        counters = [sem(n) for n in names]
        (setup, ln_bn, ln_stat, ln_root, ln_newton, ln_xn, ln_tr, ln_cp, u_mm, u_raw, u_tap, u_conv, u_act, wx_mm,
         rms_dve, rms_root, ssm_tr, ssm_cp, dl_mm, dl_act, dl_add, du_ok, g_mm, g_act,
         exp_ok, drive_ok, drive_own, scan_ok, prod_ok, sum_ok, y_half, y_ok) = counters

        with nc.Block() as credits:
            @credits.gpsimd
            def _(pool):
                for s in counters:
                    pool.sem_inc(s, CREDIT)
                for s in (u_st, y_st):
                    pool.sem_inc(s, DMA)

        block = ctx.enter_context(nc.Block())
        v2 = lambda t: t.rearrange("p (x t) -> p x t", x=2)
        hv = lambda t: t[:, :, 0:HALF]
        half = lambda x: slice(HALF * x, HALF * x + HALF)
        RMS_STEPS = 14
        first_banks = (g0, y_ps)

        def pool_drives(i, n):
            return (N - N // SHARE) * i + n + 1 - (n + 1) // SHARE

        def own_drives(i, n):
            return N // SHARE * i + (n + 1) // SHARE

        @block.sync
        def _(sp):
            for dst, src in ((w_x[:], a["w_x"]), (a_par[:], a["A"]), (conv_w[:], a["conv_w"]),
                             (conv_b, a["conv_b"]), (dt_bias, a["dt_bias"]), (d_par, a["D"]),
                             (ident[:], a["ident"])):
                sp.dma_start(dst, src).then_inc(cst_ld, DMA)
            for x, name in enumerate(("dt_ln", "b_ln", "c_ln")):
                lo, hi = (0, R, R + N, RBC)[x:x + 2]
                sp.dma_start(ln_w[:, lo:hi], a[name].partition_broadcast(P)).then_inc(cst_ld, DMA)

            def load_wu(c, place, j):
                sp.wait_ge(u_mm, done(j - 1))
                sp.dma_start(w_u[:, place], row(a["w_u"], c)).then_inc(wu_ld[place], DMA)

            def load_slot(c, place, i):
                sp.wait_ge(dl_mm, done(i - 1))
                sp.dma_start(w_dt[:, place], row(a["w_dt"], c)).then_inc(wdt_ld[place], DMA)
                sp.wait_ge(g_mm, done(2 * i - 2))
                sp.dma_start(w_g[:, place], row(a["w_g"], c)).then_inc(wg_ld[place], DMA)
                sp.wait_ge(y_st, stored(i - 1))
                sp.dma_start(u_y[:, place], row(a["u_scr"], i)).then_inc(uy_ld[place], DMA)

            def store_u(j):
                sp.wait_ge(u_act, done(j + 1))
                sp.dma_start(row(a["u_scr"], j), u_new[:]).then_inc(u_st, DMA)

            def store_y(b, c, place, i):
                sp.wait_ge(y_ok, done(i + 1))
                dst = a["y_scr"][TT * b:TT * b + TT, :, bass.ds(c, 1), :].squeeze(2).rearrange("t p k -> p t k")
                sp.dma_start(dst, u_y[:, place].rearrange("p (t k) -> p t k", t=TT)).then_inc(y_st, DMA)

            def broadcast_bc(b):
                sp.wait_ge(ssm_cp, done(2 * (b + 1)))
                sp.dma_start(a["bc_scr"][b], ssmT[R:RBC, :]).then_inc(bc_st, DMA)
                sp.wait_ge(bc_st, DMA * (b + 1))
                for g in range(4):
                    lo, hi = 4 * g, 4 * g + 4
                    k = N * (DC * b - 1) + hi
                    if b:
                        sp.wait_ge(drive_ok, done(pool_drives(DC * b - 1, hi - 1)))
                        sp.wait_ge(prod_ok, done(k))
                    sp.dma_start(b_bc[:, lo:hi, :], a["bc_scr"][b, lo:hi, :].partition_broadcast(P)).then_inc(bc_ld[g], DMA)
                    sp.dma_start(c_bc[:, lo:hi, :],
                                 a["bc_scr"][b, N + lo:N + hi, :].partition_broadcast(P)).then_inc(bc_ld[g], DMA)

            load_wu(0, 0, 0)
            load_wu(1, 1, 1)
            with sp.Fori(0, DC // 2 - 1) as c2:
                for place in range(2):
                    c = 2 * c2 + place
                    load_wu(c + 2, place, c + 2)
                    store_u(c)
            for c in range(DC - 2, DC):
                store_u(c)
            sp.wait_ge(u_st, stored(DC))
            load_slot(0, 0, 0)
            load_wu(0, 0, DC)
            broadcast_bc(0)
            for b in range(B):
                ahead = b + 1 < B

                def slot(c, place, c2, last, b=b, ahead=ahead):
                    i = c + DC * b
                    if not last:
                        load_slot(c + 1, 1 - place, i + 1)
                        if ahead:
                            load_wu(c + 1, 1 - place, i + DC + 1)
                    if ahead:
                        store_u(i + DC)
                    if ahead and last:
                        sp.wait_ge(u_st, stored(DC * (b + 2)))
                        load_slot(0, 0, DC * (b + 1))
                        if b + 2 < B:
                            load_wu(0, 0, DC * (b + 2))
                        broadcast_bc(b + 1)
                    store_y(b, c, place, i)
                over_chunks(sp, slot)
            sp.wait_ge(y_st, stored(DC * B))

        @block.scalar
        def _(act):
            def load_h(b, t):
                act.wait_ge(ln_tr, done(TT * b + t - 1))
                act.dma_start(h_t[:, (TT * b + t) % 2], a["h_all"][b, P * t:P * t + P, :]).then_inc(ht_ld[(TT * b + t) % 2], DMA)

            def root(k):
                act.wait_ge(ln_stat, done(k + 1))
                act.activation(mv[:, 3:4], mv[:, 1:2], ACT.Ln, bias=consts[:, 0:1]).then_inc(ln_root, 1)
                act.wait_ge(ln_root, done(2 * k + 1))
                act.activation(mv[:, 2:3], mv[:, 3:4], ACT.Exp, scale=-0.5).then_inc(ln_root, 1)

            def layer_norm(b):
                load_h(b, 0)
                load_h(b, 1)
                root(TT * b)
                for t in range(TT):
                    k = TT * b + t
                    if t + 1 < TT:
                        root(k + 1)
                    act.wait_ge(ln_tr, done(k + 1))
                    act.copy(xnT[:, b % 2, :, P * t:P * t + P],
                             first_banks[k % 2][:].rearrange("p x (k t) -> p (x k) t", t=P)).then_inc(ln_cp, 1)
                    if t + 2 < TT:
                        load_h(b, t + 2)

            def u_out(c, j, bank):
                act.wait_ge(u_mm, done(j + 1))
                act.wait_ge(u_conv, done(3 * j))
                act.copy(v2(raw[:, TAPS - 1:]), hv(bank)).then_inc(u_raw, 1)
                act.wait_ge(wx_mm, done(j))
                act.wait_ge(u_st, stored(j))
                act.activation(v2(u_new[:]), hv(bank), ACT.Identity, bias=conv_b[:, bass.ds(c, 1)],
                               scale=conv_w[:, bass.ds(c * TAPS + TAPS - 1, 1)]).then_inc(u_tap, 1)

            def u_silu(j):
                act.wait_ge(u_conv, done(3 * j + 3))
                act.activation(u_new[:], u_new[:], ACT.Silu).then_inc(u_act, 1)

            def softplus(step, c, place, i):
                bias = dt_bias[:, bass.ds(c, 1)]
                if step == 0:
                    act.wait_ge(dl_mm, done(i + 1))
                    act.wait_ge(du_ok, done(i - 1))
                    act.wait_ge(dl_add, done(i))
                    act.activation(v2(delta[:, place]), hv(g0), ACT.Relu, bias=bias).then_inc(dl_act, 1)
                    act.activation(v2(sp_tmp[:]), hv(g0), ACT.Abs, bias=bias).then_inc(dl_act, 1)
                elif step == 1:
                    act.wait_ge(dl_act, done(4 * i + 2))
                    act.activation(sp_tmp[:], sp_tmp[:], ACT.Exp, scale=-1.0).then_inc(dl_act, 1)
                else:
                    act.wait_ge(dl_act, done(4 * i + 3))
                    act.activation(sp_tmp[:], sp_tmp[:], ACT.Ln, bias=consts[:, 2:3]).then_inc(dl_act, 1)

            def gate(x, i):
                act.wait_ge(g_mm, done(2 * i + x + 1))
                act.wait_ge(y_ok, done(i))
                act.activation(s_gate[:, half(x)], g1[:, 0:HALF], ACT.Silu).then_inc(g_act, 1)

            def ssm_root(b):
                act.wait_ge(rms_dve, done(RMS_STEPS * b + 6))
                act.activation(ssm_t[:], ssm_ms[:], ACT.Ln, bias=consts[:, 1:2]).then_inc(rms_root, 1)
                act.wait_ge(rms_root, done(2 * b + 1))
                act.activation(ssm_r[:], ssm_t[:], ACT.Exp, scale=-0.5).then_inc(rms_root, 1)

            def ssm_out(b):
                act.wait_ge(ssm_tr, done(b + 1))
                act.copy(ssmT[:, 0:4 * P], g0[0:RBC, 0, :]).then_inc(ssm_cp, 1)
                act.copy(ssmT[:, 4 * P:], g0[0:RBC, 1, 0:P]).then_inc(ssm_cp, 1)

            act.wait_ge(setup, done(7))
            act.wait_ge(cst_ld, DMA * 10)
            layer_norm(0)
            with act.Fori(0, DC // 2) as c2:
                for place in range(2):
                    c = 2 * c2 + place
                    u_out(c, c, first_banks[place])
                    u_silu(c)
            ssm_root(0)
            ssm_out(0)
            for b in range(B):
                ahead = b + 1 < B
                for step in range(3):
                    softplus(step, 0, 0, DC * b)
                if ahead:
                    layer_norm(b + 1)

                def slot(c, place, c2, last, b=b, ahead=ahead):
                    i = c + DC * b
                    finish = ahead and last
                    for n in range(N):
                        k = N * i + n
                        if n == 0:
                            act.wait_ge(dl_add, done(i + 1))
                        act.wait_ge(scan_ok, done(k - RING_A + 1))
                        act.activation(decay[:, n % RING_A], delta[:, place], ACT.Exp,
                                       scale=a_par[:, bass.ds(c * N + n, 1)]).then_inc(exp_ok, 1)
                        if n == (8 if finish else 11) and ahead:
                            u_out(c, i + DC, g0)
                        if n == 12 and finish:
                            u_silu(i + DC)
                        if n == 15 and finish:
                            ssm_root(b + 1)
                        if n >= 13 and not last:
                            softplus(n - 13, c + 1, 1 - place, i + 1)
                        if n == (11 if finish else 14):
                            gate(0, i)
                    if ahead and not finish:
                        u_silu(i + DC)
                    gate(1, i)
                    if finish:
                        ssm_out(b + 1)
                over_chunks(act, slot)

        @block.gpsimd
        def _(pool):
            for b in range(B):
                def slot(c, place, c2, last, b=b):
                    i = c + DC * b
                    for n in range(N):
                        k = N * i + n
                        if n == 0:
                            pool.wait_ge(du_ok, done(i + 1))
                        if n % 4 == 0:
                            pool.wait_ge(bc_ld[n // 4], 2 * DMA * (b + 1))
                        if n % SHARE == SHARE - 1:
                            continue
                        pool.wait_ge(scan_ok, done(k - RING_U + 1))
                        pool.tensor_tensor(drive[:, n % RING_U], du[:, place], b_bc[:, n], ALU.mult).then_inc(drive_ok, 1)
                over_chunks(pool, slot)

        @block.vector
        def _(dve):
            def newton(v, r, t, eps, counter, at):
                dve.scalar_tensor_tensor(out=t, in0=v, scalar=eps, in1=r, op0=ALU.add, op1=ALU.mult).then_inc(counter, 1)
                dve.wait_ge(counter, done(at + 1))
                dve.tensor_tensor(t, t, r, ALU.mult).then_inc(counter, 1)
                dve.wait_ge(counter, done(at + 2))
                dve.tensor_scalar(t, t, -0.5, 1.5, ALU.mult, ALU.add).then_inc(counter, 1)
                dve.wait_ge(counter, done(at + 3))
                dve.tensor_tensor(r, r, t, ALU.mult).then_inc(counter, 1)
                dve.wait_ge(counter, done(at + 4))

            def moments(k):
                dve.wait_ge(ht_ld[k % 2], DMA * (k // 2 + 1))
                for x in range(2):
                    dve.bn_stats(stats[:, k % 2, x], h_t[:, k % 2, 512 * x:512 * x + 512]).then_inc(ln_bn, 1)

            def gather(k):
                dve.wait_ge(ln_bn, done(2 * k + 2))
                dve.wait_ge(ln_xn, done(k))
                dve.bn_aggr(mv[:, 0:2], stats[:, k % 2].rearrange("p x s -> p (x s)")).then_inc(ln_stat, 1)

            def layer_norm(b):
                moments(TT * b)
                gather(TT * b)
                for k in range(TT * b, TT * b + TT):
                    more = k + 1 < TT * b + TT
                    if more:
                        moments(k + 1)
                    dve.wait_ge(ln_root, done(2 * k + 2))
                    newton(mv[:, 1:2], mv[:, 2:3], mv[:, 3:4], LN_EPS, ln_newton, 4 * k)
                    dve.tensor_scalar(h_t[:, k % 2], h_t[:, k % 2], mv[:, 0:1], mv[:, 2:3],
                                      ALU.subtract, ALU.mult).then_inc(ln_xn, 1)
                    if more:
                        gather(k + 1)

            def conv(s, c, j):
                if s == 0:
                    dve.wait_ge(u_raw, done(j + 1))
                    dve.wait_ge(u_tap, done(j + 1))
                else:
                    dve.wait_ge(u_conv, done(3 * j + s))
                lo = TAPS - 2 - s
                dve.scalar_tensor_tensor(out=u_new[:], in0=raw[:, lo:lo + TOK],
                                         scalar=conv_w[:, bass.ds(c * TAPS + TAPS - 2 - s, 1)], in1=u_new[:],
                                         op0=ALU.mult, op1=ALU.add).then_inc(u_conv, 1)

            def step_size(place, i, uses):
                dve.wait_ge(dl_act, done(4 * i + 4))
                dve.tensor_tensor(delta[:, place], delta[:, place], sp_tmp[:], ALU.add).then_inc(dl_add, 1)
                dve.wait_ge(dl_add, done(i + 1))
                dve.wait_ge(uy_ld[place], DMA * uses)
                dve.tensor_tensor(du[:, place], delta[:, place], u_y[:, place], ALU.mult).then_inc(du_ok, 1)

            parts = ((0, R), (R, R + N), (R + N, RBC))

            def ssm_squares(b):
                at = RMS_STEPS * b
                dve.wait_ge(wx_mm, done(DC * (b + 1)))
                dve.tensor_copy(ssm[:].rearrange("p t r -> p (t r)"), ssm_ps[:, 0:TT * RBC]).then_inc(rms_dve, 1)
                dve.wait_ge(rms_dve, done(at + 1))
                dve.wait_ge(ln_tr, done(TT * (b + 1)))
                sq = h_t[:, 0, 0:TT * RBC].rearrange("p (t r) -> p t r", r=RBC)
                dve.tensor_tensor(sq, ssm[:], ssm[:], ALU.mult).then_inc(rms_dve, 1)
                dve.wait_ge(rms_dve, done(at + 2))
                for x, (lo, hi) in enumerate(parts):
                    dve.tensor_reduce(ssm_ms[:, x], sq[:, :, lo:hi], AX, ALU.add).then_inc(rms_dve, 1)
                dve.wait_ge(rms_dve, done(at + 5))
                dve.tensor_tensor(ssm_ms[:], ssm_ms[:], inv_count[:], ALU.mult).then_inc(rms_dve, 1)

            def ssm_scale(b):
                at = RMS_STEPS * b
                dve.wait_ge(rms_root, done(2 * b + 2))
                newton(ssm_ms[:], ssm_r[:], ssm_t[:], RMS_EPS, rms_dve, at + 6)
                for x, (lo, hi) in enumerate(parts):
                    dve.tensor_tensor(ssm[:, :, lo:hi], ssm[:, :, lo:hi],
                                      ssm_r[:, x].unsqueeze(2).broadcast_to([P, TT, hi - lo]), ALU.mult).then_inc(rms_dve, 1)
                dve.wait_ge(rms_dve, done(at + 13))
                dve.tensor_tensor(ssm[:], ssm[:], ln_w[:].unsqueeze(1).broadcast_to([P, TT, RBC]), ALU.mult).then_inc(rms_dve, 1)

            dve.memset(consts[:, 0:1], LN_EPS).then_inc(setup, 1)
            dve.memset(consts[:, 1:2], RMS_EPS).then_inc(setup, 1)
            dve.memset(consts[:, 2:3], 1.0).then_inc(setup, 1)
            dve.memset(inv_count[:, 0], 1.0 / R).then_inc(setup, 1)
            dve.memset(inv_count[:, 1:3], 1.0 / N).then_inc(setup, 1)
            dve.memset(zero[:], 0.0).then_inc(setup, 1)
            dve.memset(raw[:, 0:TAPS - 1], 0.0).then_inc(setup, 1)
            dve.wait_ge(cst_ld, DMA * 10)
            dve.wait_ge(setup, done(7))
            layer_norm(0)
            with dve.Fori(0, DC // 2) as c2:
                for place in range(2):
                    for s in range(TAPS - 1):
                        conv(s, 2 * c2 + place, 2 * c2 + place)
            ssm_squares(0)
            ssm_scale(0)
            for b in range(B):
                ahead = b + 1 < B
                step_size(0, DC * b, DC // 2 * b + 1)
                if ahead:
                    layer_norm(b + 1)

                def slot(c, place, c2, last, b=b, ahead=ahead):
                    i = c + DC * b
                    finish = ahead and last
                    for n in range(N):
                        k = N * i + n
                        s0 = n - (6 if finish else 9)
                        if 0 <= s0 < 3 and ahead:
                            conv(s0, c, i + DC)
                        if n == 12 and finish:
                            ssm_squares(b + 1)
                        if n == 14 and finish:
                            ssm_scale(b + 1)
                        if n == 14 and not last:
                            step_size(1 - place, i + 1, c2 + (DC // 2 * b + 1 + place))
                        if n % 4 == 0:
                            dve.wait_ge(bc_ld[n // 4], 2 * DMA * (b + 1))
                        if n % SHARE == SHARE - 1:
                            dve.tensor_tensor(drive[:, n % RING_U], du[:, place], b_bc[:, n], ALU.mult).then_inc(drive_own, 1)
                            dve.wait_ge(drive_own, done(own_drives(i, n)))
                        else:
                            dve.wait_ge(drive_ok, done(pool_drives(i, n)))
                        dve.wait_ge(exp_ok, done(k + 1))
                        dve.wait_ge(prod_ok, done(k))
                        dve.tensor_tensor_scan(state, decay[:, n % RING_A], drive[:, n % RING_U], 0.0,
                                               ALU.mult, ALU.add).then_inc(scan_ok, 1)
                        dve.wait_ge(scan_ok, done(k + 1))
                        dve.wait_ge(sum_ok, done(k - RING_C + 1))
                        dve.tensor_tensor(prod[:, n % RING_C], state, c_bc[:, n], ALU.mult).then_inc(prod_ok, 1)
                    dve.wait_ge(sum_ok, done(N * i + N))
                    dve.scalar_tensor_tensor(out=v2(u_y[:, place]), in0=v2(u_y[:, place]), scalar=d_par[:, bass.ds(c, 1)],
                                             in1=hv(y_ps), op0=ALU.mult, op1=ALU.add).then_inc(y_half, 1)
                    dve.wait_ge(y_half, done(i + 1))
                    dve.wait_ge(g_act, done(2 * i + 2))
                    dve.tensor_tensor(u_y[:, place], u_y[:, place], s_gate[:], ALU.mult).then_inc(y_ok, 1)
                over_chunks(dve, slot)

        @block.tensor
        def _(pe):
            def layer_norm(b):
                for t in range(TT):
                    k = TT * b + t
                    bank = first_banks[k % 2]
                    pe.wait_ge(ln_xn, done(k + 1))
                    pe.wait_ge(ln_cp, done(k - 1))
                    if t == 0 and b:
                        pe.wait_ge(dl_act, done(4 * DC * (b - 1) + 4))
                        pe.wait_ge(y_half, done(DC * (b - 1)))
                    for m in range(KC):
                        last = pe.transpose(bank[:, m // 4, P * (m % 4):P * (m % 4) + P], h_t[:, k % 2, P * m:P * m + P], ident[:])
                    last.then_inc(ln_tr, 1)

            def u_step(m, place, bank, xn):
                for x in range(2):
                    last = pe.matmul(bank[:, x, 0:HALF], w_u[:, place, m, :], xnT[:, xn, m, half(x)],
                                     start=(m == 0), stop=(m == KC - 1))
                if m == KC - 1:
                    last.then_inc(u_mm, 1)

            def u_first(place, c, uses):
                pe.wait_ge(wu_ld[place], DMA * uses)
                pe.wait_ge(u_tap, done(c - 1))
                for m in range(KC):
                    u_step(m, place, first_banks[place], 0)

            def gate_step(s, place, xn):
                x = s // (KC // 2)
                for m in (2 * s % KC, 2 * s % KC + 1):
                    last = pe.matmul(g1[:, 0:HALF], w_g[:, place, m, :], xnT[:, xn, m, half(x)],
                                     start=(m == 0), stop=(m == KC - 1))
                if m == KC - 1:
                    last.then_inc(g_mm, 1)

            def clear_ssm():
                pe.matmul(ssm_ps[:, 0:TT * RBC], zero[0:1, 0:P], zero[:], start=True, stop=False, skip_group_check=True)

            def wx(c, j):
                pe.wait_ge(u_act, done(j + 1))
                for t in range(TT):
                    last = pe.matmul(ssm_ps[:, RBC * t:RBC * t + RBC], u_new[:, P * t:P * t + P], w_x[:, bass.ds(c * RBC, RBC)],
                                     start=False, stop=False, skip_group_check=True)
                last.then_inc(wx_mm, 1)

            def ssm_transpose(b):
                pe.wait_ge(rms_dve, done(RMS_STEPS * (b + 1)))
                pe.wait_ge(u_tap, done(DC * (b + 1)))
                for t in range(TT):
                    last = pe.transpose(g0[0:RBC, t // 4, P * (t % 4):P * (t % 4) + P], ssm[:, t, :], ident[:])
                last.then_inc(ssm_tr, 1)

            def step_product(place, i, uses):
                pe.wait_ge(wdt_ld[place], DMA * uses)
                for x in range(2):
                    last = pe.matmul(g0[:, x, 0:HALF], w_dt[:, place, :], ssmT[0:R, half(x)], start=True, stop=True)
                last.then_inc(dl_mm, 1)

            pe.wait_ge(cst_ld, DMA * 10)
            pe.wait_ge(setup, done(7))
            layer_norm(0)
            clear_ssm()
            pe.wait_ge(ln_cp, done(TT))
            u_first(0, 0, 1)
            with pe.Fori(0, DC // 2 - 1) as c2:
                for place in range(2):
                    u_first(1 - place, 2 * c2 + place + 1, c2 + 1 + place)
                    wx(2 * c2 + place, 2 * c2 + place)
            u_first(1, DC - 1, DC // 2)
            wx(DC - 2, DC - 2)
            wx(DC - 1, DC - 1)
            ssm_transpose(0)
            for b in range(B):
                ahead = b + 1 < B
                pe.wait_ge(ssm_cp, done(2 * (b + 1)))
                step_product(0, DC * b, DC // 2 * b + 1)
                if ahead:
                    layer_norm(b + 1)
                    pe.wait_ge(rms_dve, done(RMS_STEPS * b + 1))
                    clear_ssm()
                    pe.wait_ge(ln_cp, done(TT * (b + 2)))

                def slot(c, place, c2, last, b=b, ahead=ahead):
                    i = c + DC * b
                    j = i + DC
                    finish = ahead and last
                    for n in range(N):
                        k = N * i + n
                        if n == 0 and ahead:
                            pe.wait_ge(wu_ld[place], DMA * (c2 + (DC // 2 * (b + 1) + 1)))
                            pe.wait_ge(dl_act, done(4 * i + 4))
                        if ahead:
                            for m in ((2 * n, 2 * n + 1) if finish else (0, 1) if n == 0 else (n + 1,)):
                                if m < KC:
                                    u_step(m, place, g0, (b + 1) % 2)
                        g = n - (4 if finish else 7)
                        if g == 0:
                            pe.wait_ge(wg_ld[place], DMA * (c2 + (DC // 2 * b + 1)))
                            pe.wait_ge(g_act, done(2 * i))
                        if g == KC // 2:
                            pe.wait_ge(g_act, done(2 * i + 1))
                        if 0 <= g < KC:
                            gate_step(g, place, b % 2)
                        if n == 9 and not last:
                            if ahead:
                                pe.wait_ge(u_tap, done(j + 1))
                            else:
                                pe.wait_ge(dl_act, done(4 * i + 4))
                            step_product(1 - place, i + 1, c2 + (DC // 2 * b + 1 + place))
                        if ahead and n == (11 if finish else 15):
                            wx(c, j)
                        if n == 0:
                            pe.wait_ge(y_half, done(i))
                        pe.wait_ge(prod_ok, done(k + 1))
                        for x in range(2):
                            mm = pe.matmul(y_ps[:, x, 0:HALF], ident[:], prod[:, n % RING_C, half(x)],
                                           start=(n == 0), stop=(n == N - 1))
                        mm.then_inc(sum_ok, 1)
                    if finish:
                        ssm_transpose(b + 1)
                over_chunks(pe, slot)


def output_part(nc, a, sem):
    TILES = B * TT
    with ExitStack() as ctx:
        sb = lambda name, shape: ctx.enter_context(nc.sbuf_tensor(name, shape, F32))
        pair = lambda name: [sem(f"{name}{x}") for x in range(2)]
        w_out, w_a, w_b = sb("w_out_sb", [P, DC, L]), sb("w_a_sb", [P, KC, BN]), sb("w_b_sb", [P, MC, L])
        w_q, keys = sb("w_q_sb", [P, KC, RD]), sb("keys_sb", [RD, E])
        ident = sb("o_ident", [P, P])
        y_t = sb("y_t", [P, 2, DC, P])
        h = sb("o_h", [P, 2, L])
        xn = sb("o_xn", [P, L])
        xnT = sb("o_xnT", [P, KC, P])
        zg, zgT = sb("zg", [P, BN]), sb("zgT", [P, MC, P])
        qT = sb("qT", [RD, P])
        score, left, ex = sb("score", [P, E]), sb("left", [P, 2, E]), sb("ex", [P, E])
        top = sb("top", [P, 2, 8])
        carrier = sb("carrier", [P, 5])
        scal = sb("scal", [P, 4])
        stats, mv, eps = sb("o_stats", [P, 2, 6]), sb("o_mv", [P, 4]), sb("o_eps", [P, 1])
        psum = lambda name, shape: ctx.enter_context(nc.psum_tensor(name, shape, F32))
        o_ps, t_ps, f_ps = psum("o_ps", [P, L]), psum("t_ps", [P, L]), psum("f_ps", [P, L])
        z_ps, s_ps = psum("z_ps", [P, BN]), psum("s_ps", [P, 512])

        ld, y_ld, h_ld, out_st = sem("o_ld"), pair("y_ld"), pair("h_ld"), pair("out_st")
        names = ("o_setup o_mm h2_half h2_ok o_bn o_stat o_sqrt o_rstd xn_ok xt_mm xt_cp q_mm q_cp z_mm s_mm "
                 "carried sel sel_r sel_exp zg_ok zt_mm zt_cp f_mm out_ok").split()
        counters = [sem(n) for n in names]
        (o_setup, o_mm, h2_half, h2_ok, o_bn, o_stat, o_sqrt, o_rstd, xn_ok, xt_mm, xt_cp, q_mm, q_cp, z_mm, s_mm,
         carried, sel, sel_r, sel_exp, zg_ok, zt_mm, zt_cp, f_mm, out_ok) = counters
        with nc.Block() as credits:
            @credits.gpsimd
            def _(pool):
                for s in counters:
                    pool.sem_inc(s, CREDIT)
                for s in out_st:
                    pool.sem_inc(s, DMA)
        block = ctx.enter_context(nc.Block())
        SEL = 9

        def over_tiles(eng, body):
            with eng.Fori(0, TILES // 2 - 1) as q2:
                for place in range(2):
                    body(2 * q2 + place, place, q2, False)
            for place in range(2):
                body(TILES - 2 + place, place, TILES // 2 - 1, place == 1)

        @block.sync
        def _(sp):
            for dst, src in ((w_out[:], a["w_out"]), (w_a[:], a["w_a"]), (w_b[:], a["w_b"]),
                             (w_q[:], a["w_q"]), (keys[:], a["keysT"]), (ident[:], a["ident"])):
                sp.dma_start(dst, src).then_inc(ld, DMA)

            def load(q, place):
                sp.wait_ge(o_mm, done(q - 1))
                sp.dma_start(y_t[:, place], row(a["y_scr"], q)).then_inc(y_ld[place], DMA)

            def load_h(q, place, uses):
                sp.wait_ge(out_st[place], stored(uses))
                sp.dma_start(h[:, place], row(a["h_rows"], q)).then_inc(h_ld[place], DMA)

            load(0, 0)
            load_h(0, 0, 0)

            def tile(q, place, q2, last):
                if not last:
                    load(q + 1, 1 - place)
                    load_h(q + 1, 1 - place, q2 if place == 0 else q2 + 1)
                sp.wait_ge(out_ok, done(q + 1))
                sp.dma_start(row(a["out"], q), h[:, place]).then_inc(out_st[place], DMA)
            over_tiles(sp, tile)
            for s in out_st:
                sp.wait_ge(s, stored(TILES // 2))

        @block.tensor
        def _(pe):
            def project(q, place, uses):
                pe.wait_ge(y_ld[place], DMA * uses)
                pe.wait_ge(h2_ok, done(q))
                for c in range(DC):
                    for x in range(2):
                        last = pe.matmul(o_ps[:, 512 * x:512 * x + 512], y_t[:, place, c, :], w_out[:, c, 512 * x:512 * x + 512],
                                         start=(c == 0), stop=(c == DC - 1))
                last.then_inc(o_mm, 1)

            pe.wait_ge(ld, DMA * 6)
            project(0, 0, 1)

            def tile(q, place, q2, last):
                pe.wait_ge(xn_ok, done(q + 1))
                pe.wait_ge(zt_cp, done(q))
                for m in range(KC):
                    mm = pe.transpose(t_ps[:, P * m:P * m + P], xn[:, P * m:P * m + P], ident[:])
                mm.then_inc(xt_mm, 1)
                pe.wait_ge(xt_cp, done(q + 1))
                for m in range(KC):
                    mm = pe.matmul(s_ps[0:RD, 0:P], w_q[:, m, :], xnT[:, m, :], start=(m == 0), stop=(m == KC - 1))
                mm.then_inc(q_mm, 1)
                pe.wait_ge(zg_ok, done(q))
                for m in range(KC):
                    mm = pe.matmul(z_ps[:], xnT[:, m, :], w_a[:, m, :], start=(m == 0), stop=(m == KC - 1))
                mm.then_inc(z_mm, 1)
                pe.wait_ge(q_cp, done(q + 1))
                pe.matmul(s_ps[:, P:P + E], qT[:], keys[:], start=True, stop=True).then_inc(s_mm, 1)
                if not last:
                    project(q + 1, 1 - place, (q2 + 1) if place == 0 else (q2 + 2))
                pe.wait_ge(zg_ok, done(q + 1))
                for m in range(MC):
                    mm = pe.transpose(t_ps[:, P * m:P * m + P], zg[:, P * m:P * m + P], ident[:])
                mm.then_inc(zt_mm, 1)
                pe.wait_ge(zt_cp, done(q + 1))
                pe.wait_ge(out_ok, done(q))
                for m in range(MC):
                    for x in range(2):
                        mm = pe.matmul(f_ps[:, 512 * x:512 * x + 512], zgT[:, m, :], w_b[:, m, 512 * x:512 * x + 512],
                                       start=(m == 0), stop=(m == MC - 1))
                mm.then_inc(f_mm, 1)
            over_tiles(pe, tile)

        @block.scalar
        def _(act):
            def deviation(q):
                act.wait_ge(o_stat, done(q + 1))
                act.activation(mv[:, 2:3], mv[:, 1:2], ACT.Sqrt, bias=eps[:]).then_inc(o_sqrt, 1)

            act.wait_ge(o_setup, done(1))
            deviation(0)

            def tile(q, place, q2, last):
                act.wait_ge(xt_mm, done(q + 1))
                act.wait_ge(z_mm, done(q))
                act.copy(xnT[:].rearrange("p k t -> p (k t)"), t_ps[:]).then_inc(xt_cp, 1)
                act.wait_ge(q_mm, done(q + 1))
                act.copy(qT[:], s_ps[0:RD, 0:P]).then_inc(q_cp, 1)
                act.wait_ge(sel, done(SEL * q + 3))
                act.activation(ex[:], score[:], ACT.Exp, bias=scal[:, 0:1]).then_inc(sel_exp, 1)
                if not last:
                    deviation(q + 1)
                act.wait_ge(zt_mm, done(q + 1))
                act.wait_ge(f_mm, done(q))
                act.copy(zgT[:].rearrange("p m t -> p (m t)"), t_ps[:, 0:BN]).then_inc(zt_cp, 1)
            over_tiles(act, tile)

        @block.vector
        def _(dve):
            def front(q, place, uses):
                dve.wait_ge(o_mm, done(q + 1))
                dve.wait_ge(h_ld[place], DMA * uses)
                dve.tensor_tensor(h[:, place], h[:, place], o_ps[:], ALU.add).then_inc(h2_ok, 1)
                dve.wait_ge(h2_ok, done(q + 1))
                for x in range(2):
                    dve.bn_stats(stats[:, x], h[:, place, 512 * x:512 * x + 512]).then_inc(o_bn, 1)
                dve.wait_ge(o_bn, done(2 * q + 2))
                dve.tensor_copy(carrier[:, 0:1], stats[:, 0, 0:1]).then_inc(carried, 1)
                dve.bn_aggr(mv[:, 0:2], stats[:].rearrange("p x s -> p (x s)")).then_inc(o_stat, 1)
                dve.wait_ge(o_sqrt, done(q + 1))
                dve.reciprocal(mv[:, 3:4], mv[:, 2:3]).then_inc(o_rstd, 1)
                dve.wait_ge(o_rstd, done(q + 1))
                dve.wait_ge(xt_mm, done(q))
                dve.tensor_scalar(xn[:], h[:, place], mv[:, 0:1], mv[:, 3:4], ALU.subtract, ALU.mult).then_inc(xn_ok, 1)

            dve.memset(eps[:], LN_EPS).then_inc(o_setup, 1)
            front(0, 0, 1)

            def tile(q, place, q2, last):
                at = q * SEL

                def link(step, ins):
                    ins.then_inc(sel, 1)
                    dve.wait_ge(sel, done(at + step))

                dve.wait_ge(s_mm, done(q + 1))
                link(1, dve.tensor_copy(score[:], s_ps[:, P:P + E]))
                dve.tensor_copy(carrier[:, 1:2], score[:, 0:1]).then_inc(carried, 1)
                link(2, dve.max(top[:, 0], score[:]))
                link(3, dve.tensor_scalar(scal[:, 0:1], top[:, 0, 0:1], -1.0, None, ALU.mult))
                dve.tensor_copy(carrier[:, 2:3], scal[:, 0:1]).then_inc(carried, 1)
                link(4, dve.match_replace(left[:, 0], top[:, 0], score[:], -3.0e38))
                dve.tensor_copy(carrier[:, 3:4], left[:, 0, 0:1]).then_inc(carried, 1)
                link(5, dve.max(top[:, 1], left[:, 0]))
                dve.tensor_copy(carrier[:, 4:5], top[:, 1, 0:1]).then_inc(carried, 1)
                link(6, dve.match_replace(left[:, 1], top[:, 1], left[:, 0], -3.0e38))
                link(7, dve.tensor_tensor(left[:, 0], score[:], left[:, 1], ALU.not_equal))
                dve.wait_ge(sel_exp, done(q + 1))
                link(8, dve.tensor_tensor(ex[:], ex[:], left[:, 0], ALU.mult))
                dve.tensor_reduce(scal[:, 1:2], ex[:], AX, ALU.add).then_inc(sel, 1)
                dve.wait_ge(sel, done(at + 9))
                dve.reciprocal(scal[:, 2:3], scal[:, 1:2]).then_inc(sel_r, 1)
                dve.wait_ge(sel_r, done(2 * q + 1))
                dve.tensor_scalar(ex[:], ex[:], scal[:, 2:3], 2.0, ALU.mult, ALU.mult).then_inc(sel_r, 1)
                dve.wait_ge(sel_r, done(2 * q + 2))
                dve.wait_ge(z_mm, done(q + 1))
                dve.wait_ge(zt_mm, done(q))
                dve.tensor_tensor(zg[:].rearrange("p (e r) -> p e r", e=E), z_ps[:].rearrange("p (e r) -> p e r", e=E),
                                  ex[:].unsqueeze(2).broadcast_to([P, E, RANK]), ALU.mult).then_inc(zg_ok, 1)
                if not last:
                    front(q + 1, 1 - place, (q2 + 1) if place == 0 else (q2 + 2))
                dve.wait_ge(f_mm, done(q + 1))
                dve.tensor_tensor(h[:, place], h[:, place], f_ps[:], ALU.add).then_inc(out_ok, 1)
            over_tiles(dve, tile)


def build(nc, a):
    with ExitStack() as ctx:
        sem = lambda name: ctx.enter_context(nc.semaphore(name))
        tokens_part(nc, a, sem)
        mixer_part(nc, a, sem)
        output_part(nc, a, sem)


def constants():
    t = np.zeros((P, NV + 8), np.float32)
    t[:, 0:NA] = 64 * np.arange(NA)
    t[:, NA:NA + NB1] = NB2 * np.arange(NB1)
    t[:, NA + NB1:NV] = np.arange(NB2)
    re = np.arange(P) < 64
    t[:, NV] = np.where(re, 0.25, 0)
    t[:, NV + 1] = np.where(re, 0, 0.25)
    t[:, NV + 2] = np.where(re, np.pi / 2, 0)
    t[:, NV + 3] = np.where(re, 0, np.pi / 2)
    t[:, NV + 4] = np.where(re, 1, -1)
    t[:, NV + 5] = -t[:, NV + 4]
    return t


def layouts(x):
    cont = np.ascontiguousarray
    per_chunk = lambda v, w: cont(v.reshape(DC, P, w).transpose(1, 0, 2).reshape(P, DC * w))
    lhs = lambda w: cont(w.reshape(DC, P, KC, P).transpose(0, 3, 2, 1))
    rhs = lambda w, k: cont(w.T.reshape(k, P, w.shape[0]).transpose(1, 0, 2))
    s4, w_in = x["x"], x["L0_attn_W_in"]
    return {
        "aimT": cont(x["L0_tok_A_imag"].T), "iarT": cont(x["L0_tok_inv_A_real"].T),
        "brT": cont(x["L0_tok_B"][..., 0].T), "biT": cont(x["L0_tok_B"][..., 1].T),
        "crT": cont(s4[..., 0].transpose(2, 0, 1)), "ciT": cont(s4[..., 1].transpose(2, 0, 1)),
        "log_dt": x["L0_tok_log_dt"], "txt": x["txt"],
        "w_u": lhs(w_in[:D]), "w_g": lhs(w_in[D:]),
        "w_dt": cont(x["L0_attn_Wdt"].reshape(DC, P, R).transpose(0, 2, 1)),
        "w_x": rhs(x["L0_attn_Wx"], DC).reshape(P, DC * RBC),
        "A": per_chunk(x["L0_attn_A"], N), "conv_w": per_chunk(x["L0_attn_conv_w"], TAPS),
        "conv_b": per_chunk(x["L0_attn_conv_b"], 1), "dt_bias": per_chunk(x["L0_attn_dt_bias"], 1),
        "D": per_chunk(x["L0_attn_D_param"], 1),
        "dt_ln": x["L0_attn_dt_ln_w"], "b_ln": x["L0_attn_b_ln_w"], "c_ln": x["L0_attn_c_ln_w"],
        "w_out": rhs(x["L0_attn_W_out"], DC), "w_a": rhs(x["L0_ffn_A_w"], KC), "w_b": rhs(x["L0_ffn_B_w"], MC),
        "w_q": rhs(x["L0_ffn_Wq_w"], KC), "keysT": cont(x["L0_ffn_keys"].T),
        "cst": constants(), "ident": np.eye(P, dtype=np.float32),
    }


def kernel(**inputs):
    import concourse.bacc as bacc
    from concourse.bass_utils import run_bass_kernel_spmd

    nc = bacc.Bacc("TRN2", target_bir_lowering=False, num_devices=1)
    arrays = layouts({k: np.asarray(v) for k, v in inputs.items()})
    a = {k: nc.dram_tensor(f"in_{k}", v.shape, F32, kind="ExternalInput").ap() for k, v in arrays.items()}
    for name, shape in (("h_all", [B, TOK, L]), ("u_scr", [B * DC, P, TOK]), ("y_scr", [B * TT, P, DC, P]),
                        ("bc_scr", [B, 2 * N, TOK])):
        a[name] = nc.dram_tensor(name, shape, F32, kind="Internal").ap()
    out = nc.dram_tensor("out", [B, TOK, L], F32, kind="ExternalOutput").ap()
    tiles = lambda t: t.rearrange("b (t p) l -> (b t) p l", p=P)
    a["h_rows"], a["out"] = tiles(a["h_all"]), tiles(out)
    build(nc, a)
    r = run_bass_kernel_spmd(nc, [{f"in_{k}": v for k, v in arrays.items()}], core_ids=[0])
    return r.results[0]["out"]
```

```python
import numpy as np
from contextlib import ExitStack

import concourse.bass as bass
from concourse import mybir

P = 128
F32 = mybir.dt.float32
F32R = mybir.dt.float32r
ALU = mybir.AluOpType
ACT = mybir.ActivationFunctionType
AX = mybir.AxisListType.X

B = 4
HS, NS = 128, 64
L = 1024
KC = L // P
TOK = 640
TT = TOK // P
HALF = TOK // 2
D = 2048
DC = D // P
N = 16
R = 64
RBC = R + 2 * N
TAPS = 4
E = 64
RANK = 8
RD = 16
BN = E * RANK
MC = BN // P

NA, NB1, NB2 = 16, 8, 8
NV = NA + NB1 + NB2
TWO_PI_HI = 6.28125
TWO_PI_MID = 0.0019350051879882812
TWO_PI_LO = 2 * np.pi - TWO_PI_HI - TWO_PI_MID
ROUND = 1.5 * 2.0 ** 23
PI_MAX = 3.1415925
LN_EPS = 1e-5
RMS_EPS = 1e-6


def tokens_part(nc, a, sem):
    with ExitStack() as ctx:
        sb = lambda name, shape: ctx.enter_context(nc.sbuf_tensor(name, shape, F32))
        cst = sb("t_cst", [P, NV + 4])
        aim, iar, br, bi, ldt = (sb(f"t_{x}", [P, HS]) for x in ("aim", "iar", "br", "bi", "ldt"))
        cr, ci = sb("t_cr", [P, B, HS]), sb("t_ci", [P, B, HS])
        small = {x: sb(f"t_s_{x}", [P, HS]) for x in (
            "are", "dt", "zr", "zi", "den", "rden", "inr", "ini", "nr", "p0", "p1", "mr", "mi", "gr", "gi", "gb", "gbn")}
        two = sb("t_two", [P, 2, HS, NV])
        th, kk = two[:, 0], two[:, 1]
        mag = sb("t_mag", [P, HS, NV])
        own, swp = sb("t_own", [P, HS, NV]), sb("t_swp", [P, HS, NV])
        h_re, h_im, h_sg = (sb(f"t_h{x}", [P, HS, NB2]) for x in ("re", "im", "sg"))
        e2 = sb("t_e2", [P, HS, NB1 * NB2])
        q_own, q_swp, q_tmp = (sb(f"t_q{x}", [P, HS, NA]) for x in ("own", "swp", "tmp"))
        ca, cb = sb("t_ca", [P, HS, B]), sb("t_cb", [P, HS, B])
        w = sb("t_w", [P, HS, B * NA])
        tmp = two[:].rearrange("p x h v -> p (x h v)").rearrange("p (h v) -> p h v", h=HS)
        kout = mag[:].rearrange("p h v -> p (h v)").rearrange("p (h v) -> p h v", h=HS // 2)
        ps = [ctx.enter_context(nc.psum_tensor(f"t_ps{g}", [P, 8, 64], F32)) for g in range(8)]
        ld, dv, ac, mm, ev, st = (sem(f"t_{x}") for x in ("ld", "dv", "ac", "mm", "ev", "st"))
        marks = {}
        block = ctx.enter_context(nc.Block())

        lv = cst[:, 0:NV]
        turns, quarter_turn, sgn, nsgn = (cst[:, NV + x:NV + x + 1] for x in range(4))

        def over_v(x, n):
            return x.unsqueeze(2).broadcast_to([P, HS, n])

        @block.sync
        def _(sp):
            n = 0
            for half in range(2):
                rows = slice(64 * half, 64 * half + 64)
                for dst, src in ((aim, a["aimT"]), (iar, a["iarT"]), (br, a["brT"]), (bi, a["biT"])):
                    sp.dma_start(dst[rows, :], src).then_inc(ld, 16)
                sp.dma_start(cr[rows, :, :], a["crT"]).then_inc(ld, 16)
                sp.dma_start(ci[rows, :, :], a["ciT"]).then_inc(ld, 16)
                n += 6
            sp.dma_start(ldt[:, :], a["log_dt"].partition_broadcast(P)).then_inc(ld, 16)
            sp.dma_start(cst[:, :], a["cst"]).then_inc(ld, 16)
            assert n + 2 == 14
            for c in range(B):
                sp.dma_start(a["h_all"][c, P:TOK, :], a["txt"][c]).then_inc(st, 16)
            sp.wait_ge(ev, 8)
            for hh in range(2):
                for c in range(B):
                    p0 = 64 * hh + NA * c
                    dst = a["h_all"][c, 64 * hh:64 * hh + 64, :].rearrange("h (a b) -> a h b", a=NA)
                    sp.dma_start(dst, kout[p0:p0 + NA, :, :]).then_inc(st, 16)
            sp.wait_ge(st, 16 * 12)

        count = [0]
        marks_mag = 4
        marks_arg = (12, 15)

        @block.scalar
        def _(act):
            act.wait_ge(ld, 16 * 14)
            act.activation(small["dt"][:], ldt[:], ACT.Exp).then_inc(ac, 1)
            act.activation(small["are"][:], iar[:], ACT.Exp).then_inc(ac, 1)
            act.wait_ge(dv, marks_mag)
            act.activation(mag[:], mag[:], ACT.Exp).then_inc(ac, 1)
            act.wait_ge(dv, marks_arg[0])
            act.activation(own[:], own[:], ACT.Sin).then_inc(ac, 1)
            act.wait_ge(dv, marks_arg[1])
            act.activation(swp[:], swp[:], ACT.Sin, scale=nsgn).then_inc(ac, 1)

        @block.vector
        def _(dve):
            def link(ins):
                count[0] += 1
                ins.then_inc(dv, 1)
                dve.wait_ge(dv, count[0])

            s = small
            dve.wait_ge(ac, 2)
            dve.wait_ge(ld, 16 * 14)
            link(dve.scalar_tensor_tensor(out=s["zr"][:], in0=s["are"][:], scalar=-1.0, in1=s["dt"][:],
                                          op0=ALU.mult, op1=ALU.mult))
            link(dve.tensor_tensor(s["zi"][:], aim[:], s["dt"][:], ALU.mult))
            lvb = lv.unsqueeze(1).broadcast_to([P, HS, NV])
            link(dve.tensor_tensor(th, over_v(s["zi"][:], NV), lvb, ALU.mult))
            link(dve.tensor_tensor(mag[:], over_v(s["zr"][:], NV), lvb, ALU.mult))
            assert count[0] == marks_mag
            link(dve.tensor_scalar(kk, th, float(1 / (2 * np.pi)), turns, ALU.mult, ALU.add))
            link(dve.tensor_scalar(kk, kk, ROUND, -ROUND, ALU.add, ALU.add))
            link(dve.scalar_tensor_tensor(out=own[:], in0=kk, scalar=-TWO_PI_HI, in1=th, op0=ALU.mult, op1=ALU.add))
            link(dve.scalar_tensor_tensor(out=own[:], in0=kk, scalar=-TWO_PI_MID, in1=own[:], op0=ALU.mult, op1=ALU.add))
            link(dve.scalar_tensor_tensor(out=own[:], in0=kk, scalar=-TWO_PI_LO, in1=own[:], op0=ALU.mult, op1=ALU.add))
            link(dve.tensor_scalar(own[:], own[:], quarter_turn, PI_MAX, ALU.add, ALU.min))
            link(dve.tensor_scalar(own[:], own[:], -PI_MAX, None, ALU.max))
            link(dve.tensor_scalar(swp[:], own[:], nsgn, float(np.pi / 2), ALU.mult, ALU.add))
            assert count[0] == marks_arg[0]
            link(dve.tensor_scalar(kk, swp[:], PI_MAX, float(-2 * np.pi), ALU.is_gt, ALU.mult))
            link(dve.tensor_tensor(swp[:], swp[:], kk, ALU.add))
            link(dve.tensor_scalar(swp[:], swp[:], -PI_MAX, PI_MAX, ALU.max, ALU.min))
            assert count[0] == marks_arg[1]
            for x, t in enumerate((own, swp)):
                dve.wait_ge(ac, 4 + x)
                link(dve.tensor_tensor(t[:], t[:], mag[:], ALU.mult))
            lo, hi = slice(0, 64), slice(64, P)
            v2 = slice(NA + NB1, NV)
            for dst, first, second in ((h_re, own, swp), (h_im, swp, own)):
                link(dve.tensor_copy(dst[lo, :, :], first[lo, :, v2]))
                link(dve.tensor_copy(dst[hi, :, :], second[hi, :, v2]))
            link(dve.tensor_scalar(h_sg[:], h_im[:], nsgn, None, ALU.mult))
            shape = [P, HS, NB1, NB2]
            e2v = e2[:].rearrange("p h (x y) -> p h x y", x=NB1)
            tmpv = tmp.rearrange("p h (x y) -> p h x y", x=NB1)
            b1 = slice(NA, NA + NB1)
            link(dve.tensor_tensor(e2v, own[:, :, b1].unsqueeze(3).broadcast_to(shape),
                                   h_re[:].unsqueeze(2).broadcast_to(shape), ALU.mult))
            link(dve.tensor_tensor(tmpv, swp[:, :, b1].unsqueeze(3).broadcast_to(shape),
                                   h_sg[:].unsqueeze(2).broadcast_to(shape), ALU.mult))
            link(dve.tensor_tensor(e2[:], e2[:], tmp, ALU.add))
            tt = lambda o, x, y, op: link(dve.tensor_tensor(s[o][:], x, y, op))
            tt("den", s["are"][:], s["are"][:], ALU.mult)
            tt("p0", aim[:], aim[:], ALU.mult)
            tt("den", s["den"][:], s["p0"][:], ALU.add)
            link(dve.reciprocal(s["rden"][:], s["den"][:]))
            link(dve.scalar_tensor_tensor(out=s["inr"][:], in0=s["are"][:], scalar=-1.0, in1=s["rden"][:],
                                          op0=ALU.mult, op1=ALU.mult))
            link(dve.scalar_tensor_tensor(out=s["ini"][:], in0=aim[:], scalar=-1.0, in1=s["rden"][:],
                                          op0=ALU.mult, op1=ALU.mult))
            link(dve.tensor_scalar(s["nr"][:], h_re[:, :, 1], -1.0, None, ALU.add))
            ni = h_im[:, :, 1]

            def complex_product(ore, oim, xr, xi, yr, yi):
                tt("p0", xr, yr, ALU.mult)
                tt("p1", xi, yi, ALU.mult)
                tt(ore, s["p0"][:], s["p1"][:], ALU.subtract)
                tt("p0", xr, yi, ALU.mult)
                tt("p1", xi, yr, ALU.mult)
                tt(oim, s["p0"][:], s["p1"][:], ALU.add)

            complex_product("mr", "mi", s["nr"][:], ni, s["inr"][:], s["ini"][:])
            complex_product("gr", "gi", br[:], bi[:], s["mr"][:], s["mi"][:])
            link(dve.tensor_scalar(s["gr"][:], s["gr"][:], 2.0, None, ALU.mult))
            link(dve.tensor_scalar(s["gb"][:], s["gi"][:], nsgn, 2.0, ALU.mult, ALU.mult))
            link(dve.tensor_scalar(s["gbn"][:], s["gb"][:], -1.0, None, ALU.mult))
            va = slice(0, NA)
            for dst, first, second, g2 in ((q_own, own, swp, "gb"), (q_swp, swp, own, "gbn")):
                link(dve.tensor_tensor(dst[:], first[:, :, va], over_v(s["gr"][:], NA), ALU.mult))
                link(dve.tensor_tensor(q_tmp[:], second[:, :, va], over_v(s[g2][:], NA), ALU.mult))
                link(dve.tensor_tensor(dst[:], dst[:], q_tmp[:], ALU.add))
            link(dve.tensor_scalar(ca[:].rearrange("p h c -> p c h"), cr[:], sgn, None, ALU.mult))
            link(dve.tensor_scalar(cb[:].rearrange("p h c -> p c h"), ci[:], -1.0, None, ALU.mult))
            wv = w[:].rearrange("p h (c x) -> p h c x", c=B)
            tmpw = tmp.rearrange("p h (c x) -> p h c x", c=B)
            quarter = HS // 4
            shape = [P, quarter, B, NA]
            for first in range(2):
                for hh in range(2):
                    hs = slice(64 * hh + quarter * first, 64 * hh + quarter * (first + 1))
                    link(dve.tensor_tensor(wv[:, hs], q_own[:, hs].unsqueeze(2).broadcast_to(shape),
                                           ca[:, hs].unsqueeze(3).broadcast_to(shape), ALU.mult))
                    link(dve.tensor_tensor(tmpw[:, hs], q_swp[:, hs].unsqueeze(2).broadcast_to(shape),
                                           cb[:, hs].unsqueeze(3).broadcast_to(shape), ALU.mult))
                    link(dve.tensor_tensor(w[:, hs], w[:, hs], tmp[:, hs], ALU.add))
                marks["w", first] = count[0]
            for g in range(8):
                dve.wait_ge(mm, g + 1)
                dve.tensor_copy(kout[:, 8 * g:8 * g + 8, :], ps[g][:]).then_inc(ev, 1)

        @block.tensor
        def _(pe):
            for g in range(8):
                if g % 4 == 0:
                    pe.wait_ge(dv, marks["w", g // 4])
                for x in range(8):
                    for hh in range(2):
                        h = 64 * hh + 8 * g + x
                        last = pe.matmul(ps[g][64 * hh:64 * hh + 64, x, :], w[:, h, :], e2[:, h, :],
                                         start=True, stop=True)
                last.then_inc(mm, 1)


CREDIT = 8
DMA = 16
RING_A, RING_U, RING_C = 4, 2, 3
BC_FROM = (0, 2, 4, 8, 12)


def own_steps(b):
    return (5, 10, 15) if b + 1 < B else range(7, N, 8)


def own_drives(b, c, n):
    return len(own_steps(b)) * c + (DC * sum(len(own_steps(x)) for x in range(b)) + sum(x <= n for x in own_steps(b)))


def pool_drives(b, c, n):
    others = [N - len(own_steps(x)) for x in range(b + 1)]
    return others[b] * c + (DC * sum(others[:b]) + n + 1 - sum(x <= n for x in own_steps(b)))


def done(count):
    return count + CREDIT


def stored(count):
    return DMA * count + DMA


def over_chunks(eng, body):
    with eng.Fori(0, DC // 2 - 1) as c2:
        for place in range(2):
            body(2 * c2 + place, place, c2, False)
    for place in range(2):
        body(DC - 2 + place, place, DC // 2 - 1, place == 1)


def newton_step(dve, v, r, t, eps, counter, at):
    dve.scalar_tensor_tensor(out=t, in0=v, scalar=eps, in1=r, op0=ALU.add, op1=ALU.mult).then_inc(counter, 1)
    dve.wait_ge(counter, done(at + 1))
    dve.tensor_tensor(t, t, r, ALU.mult).then_inc(counter, 1)
    dve.wait_ge(counter, done(at + 2))
    dve.tensor_scalar(t, t, -0.5, 1.5, ALU.mult, ALU.add).then_inc(counter, 1)
    dve.wait_ge(counter, done(at + 3))
    dve.tensor_tensor(r, r, t, ALU.mult).then_inc(counter, 1)
    dve.wait_ge(counter, done(at + 4))


def row(t, i):
    return t[bass.ds(i, 1)].squeeze(0)


def mixer_part(nc, a, sem):
    with ExitStack() as ctx:
        sb = lambda name, shape: ctx.enter_context(nc.sbuf_tensor(name, shape, F32))
        pair = lambda name: [sem(f"{name}{x}") for x in range(2)]

        b_bc, c_bc = sb("b_bc", [P, N, TOK]), sb("c_bc", [P, N, TOK])
        xnT = sb("xnT", [P, 2, KC, TOK])
        decay = sb("decay", [P, RING_A, TOK])
        drive = sb("drive", [P, RING_U, TOK])
        prod = sb("prod", [P, RING_C, TOK])
        u_new = sb("u_new", [P, TOK])
        raw = sb("raw", [P, TAPS - 1 + TOK])
        u_y = sb("u_y", [P, 2, TOK])
        delta = sb("delta", [P, 2, TOK])
        du = sb("du", [P, 2, TOK])
        s_gate = sb("s_gate", [P, TOK])
        sp_tmp = sb("sp_tmp", [P, TOK])
        ssmT = sb("ssmT", [RBC, TOK])
        w_u = sb("w_u_sb", [P, 2, KC, P])
        w_g = sb("w_g_sb", [P, 2, KC, P])
        w_dt = sb("w_dt_sb", [R, 2, P])
        w_x = sb("w_x_sb", [P, DC * RBC])
        a_par = sb("a_par", [P, DC * N])
        conv_w = sb("conv_w_sb", [P, DC * TAPS])
        vec = sb("vec", [P, 3 * DC])
        conv_b, dt_bias, d_par = (vec[:, DC * x:DC * x + DC] for x in range(3))
        ln_w = sb("ln_w", [P, RBC])
        ident = sb("ident_sb", [P, P])
        h_t = sb("h_t", [P, 2, L])
        stats = sb("stats", [P, 2, 2, 6])
        mv = sb("mv", [P, 4])
        carrier = sb("ln_carrier", [P, 1])
        ssm = sb("ssm", [P, TT, RBC])
        ssm_ms = sb("ssm_ms", [P, 3, TT])
        ssm_r = sb("ssm_r", [P, 3, TT])
        ssm_t = sb("ssm_t", [P, 3, TT])
        inv_count = sb("inv_count", [P, 3, TT])
        consts = sb("consts", [P, 3])
        zero = sb("zero", [1, P])

        bank_pair = lambda name: ctx.enter_context(nc.psum_tensor(name, [P, 2, 512], F32))
        y_ps, g0, state_ps = bank_pair("y_ps"), bank_pair("g0"), bank_pair("state_ps")
        STATES = 3
        states = state_ps[:].rearrange("p x t -> p (x t)")[:, 0:STATES * HALF].rearrange("p (s t) -> p s t", t=HALF)
        g1 = ctx.enter_context(nc.psum_tensor("g1", [P, 512], F32))
        ssm_ps = ctx.enter_context(nc.psum_tensor("ssm_ps", [P, 512], F32))

        h_first = b_bc[:].rearrange("p n t -> p (n t)")
        xn_out = decay[:].rearrange("p a t -> p (a t)")

        id_ld, cst_ld, ht_ld, bc_st = sem("id_ld"), sem("cst_ld"), pair("ht_ld"), sem("bc_st")
        h0_ld = [sem(f"h0_ld{t}") for t in range(TT)]
        xn_st, xn_ld = pair("xn_st"), sem("xn_ld")
        wu_ld, wg_ld, wdt_ld, uy_ld = pair("wu_ld"), pair("wg_ld"), pair("wdt_ld"), pair("uy_ld")
        bc_ld = [sem(f"bc_ld{g}") for g in range(len(BC_FROM))]
        u_st, y_st = pair("u_st"), sem("y_st")
        names = ("setup ln_bn ln_stat ln_root ln_newton ln_xn ln_tr ln_cp u_mm u_raw u_tap u_conv u_sig u_act wx_mm "
                 "rms_dve rms_root ssm_tr ssm_cp dl_mm dl_act dl_add du_ok g_mm g_act g_sig "
                 "exp_ok drive_ok drive_own scan_ok prod_ok sum_ok y_half y_gate y_ok ln_carried").split()
        counters = [sem(n) for n in names]
        (setup, ln_bn, ln_stat, ln_root, ln_newton, ln_xn, ln_tr, ln_cp, u_mm, u_raw, u_tap, u_conv, u_sig, u_act, wx_mm,
         rms_dve, rms_root, ssm_tr, ssm_cp, dl_mm, dl_act, dl_add, du_ok, g_mm, g_act, g_sig,
         exp_ok, drive_ok, drive_own, scan_ok, prod_ok, sum_ok, y_half, y_gate, y_ok, ln_carried) = counters

        with nc.Block() as credits:
            @credits.gpsimd
            def _(pool):
                for s in counters:
                    pool.sem_inc(s, CREDIT)
                for s in (*u_st, y_st, *xn_st):
                    pool.sem_inc(s, DMA)

        block = ctx.enter_context(nc.Block())
        v2 = lambda t: t.rearrange("p (x t) -> p x t", x=2)
        hv = lambda t: t[:, :, 0:HALF]
        half = lambda x: slice(HALF * x, HALF * x + HALF)
        RMS_STEPS = 14
        first_banks = (g0, y_ps)

        def h_at(k, place):
            return h_first[:, L * k:L * k + L] if place is None else h_t[:, place]

        u_first_tiles = (u_new[:], du[:, 0])

        def over_first(eng, body):
            with eng.Fori(0, DC // 2 - 2) as c2:
                for place in range(2):
                    body(2 * c2 + place, place, c2, True)
            for c in range(DC - 4, DC):
                body(c, c % 2, c // 2, c + TT < B * TT)

        @block.sync
        def _(sp):
            sp.dma_start(ident[:], a["ident"]).then_inc(id_ld, DMA)
            for t in range(TT):
                sp.dma_start(h_at(t, None), row(a["h_rows"], t)).then_inc(h0_ld[t], DMA)

            def load_wu(c, place, j):
                sp.wait_ge(u_mm, done(j - 1))
                sp.dma_start(w_u[:, place], row(a["w_u"], c)).then_inc(wu_ld[place], DMA)

            def load_slot(c, place, i):
                sp.wait_ge(dl_mm, done(i - 1))
                sp.dma_start(w_dt[:, place], row(a["w_dt"], c)).then_inc(wdt_ld[place], DMA)
                sp.wait_ge(g_mm, done(2 * i - 2))
                sp.dma_start(w_g[:, place], row(a["w_g"], c)).then_inc(wg_ld[place], DMA)
                sp.wait_ge(y_st, stored(i - 1))
                sp.dma_start(u_y[:, place], row(a["u_scr"], i)).then_inc(uy_ld[place], DMA)

            def store_u(j, place, u):
                sp.wait_ge(u_act, done(j + 1))
                sp.dma_start(row(a["u_scr"], j), u).then_inc(u_st[place], DMA)

            def store_y(b, c, place, i):
                sp.wait_ge(y_ok, done(i + 1))
                dst = a["y_scr"][TT * b:TT * b + TT, :, bass.ds(c, 1), :].squeeze(2).rearrange("t p k -> p t k")
                sp.dma_start(dst, u_y[:, place].rearrange("p (t k) -> p t k", t=TT)).then_inc(y_st, DMA)

            def broadcast_bc(b):
                sp.wait_ge(ssm_cp, done(2 * (b + 1)))
                sp.dma_start(a["bc_scr"][b], ssmT[R:RBC, :]).then_inc(bc_st, DMA)
                sp.wait_ge(bc_st, DMA * (b + 1))
                for g, (lo, hi) in enumerate(zip(BC_FROM, (*BC_FROM[1:], N))):
                    k = N * (DC * b - 1) + hi
                    if b:
                        sp.wait_ge(drive_ok, done(pool_drives(b - 1, DC - 1, hi - 1)))
                        sp.wait_ge(prod_ok, done(2 * k))
                    sp.dma_start(b_bc[:, lo:hi, :], a["bc_scr"][b, lo:hi, :].partition_broadcast(P)).then_inc(bc_ld[g], DMA)
                    sp.dma_start(c_bc[:, lo:hi, :],
                                 a["bc_scr"][b, N + lo:N + hi, :].partition_broadcast(P)).then_inc(bc_ld[g], DMA)

            def load_xn(b):
                for t in range(TT):
                    sp.dma_start(xnT[:, b % 2, :, P * t:P * t + P], a["xn_scr"][TT * b + t]).then_inc(xn_ld, DMA)

            load_wu(0, 0, 0)
            for dst, src in ((conv_w[:], a["conv_w"]), (conv_b, a["conv_b"]), (w_x[:], a["w_x"]), (a_par[:], a["A"]),
                             (dt_bias, a["dt_bias"]), (d_par, a["D"])):
                sp.dma_start(dst, src).then_inc(cst_ld, DMA)
            for x, name in enumerate(("dt_ln", "b_ln", "c_ln")):
                lo, hi = (0, R, R + N, RBC)[x:x + 2]
                sp.dma_start(ln_w[:, lo:hi], a[name].partition_broadcast(P)).then_inc(cst_ld, DMA)
            load_wu(1, 1, 1)
            with sp.Fori(0, DC // 2 - 1) as c2:
                for place in range(2):
                    c = 2 * c2 + place
                    load_wu(c + 2, place, c + 2)
                    store_u(c, place, u_first_tiles[place])
            for c in range(DC - 2, DC):
                store_u(c, c % 2, u_first_tiles[c % 2])
            for s in u_st:
                sp.wait_ge(s, stored(DC // 2))
            load_slot(0, 0, 0)
            load_wu(0, 0, DC)
            sp.wait_ge(xn_st[0], stored((B * TT - TT) // 2))
            sp.wait_ge(xn_st[1], stored((B * TT - TT + 1) // 2))
            load_xn(1)
            broadcast_bc(0)
            for b in range(B):
                ahead = b + 1 < B

                def slot(c, place, c2, last, b=b, ahead=ahead):
                    i = c + DC * b
                    if not last:
                        load_slot(c + 1, 1 - place, i + 1)
                        if ahead:
                            load_wu(c + 1, 1 - place, i + DC + 1)
                    if ahead:
                        store_u(i + DC, place, u_new[:])
                    if ahead and last:
                        for s in u_st:
                            sp.wait_ge(s, stored(DC // 2 * (b + 2)))
                        load_slot(0, 0, DC * (b + 1))
                        if b + 2 < B:
                            load_wu(0, 0, DC * (b + 2))
                            sp.wait_ge(g_mm, done(2 * DC * (b + 1)))
                            load_xn(b + 2)
                        broadcast_bc(b + 1)
                    store_y(b, c, place, i)
                over_chunks(sp, slot)
            sp.wait_ge(y_st, stored(DC * B))

        @block.scalar
        def _(act):
            def load_h(k, place):
                act.dma_start(h_t[:, place], row(a["h_rows"], k)).then_inc(ht_ld[place], DMA)

            def root(k):
                act.wait_ge(ln_stat, done(k + 1))
                act.activation(mv[:, 3:4], mv[:, 1:2], ACT.Ln, bias=consts[:, 0:1]).then_inc(ln_root, 1)
                act.wait_ge(ln_root, done(2 * k + 1))
                act.activation(mv[:, 2:3], mv[:, 3:4], ACT.Exp, scale=-0.5).then_inc(ln_root, 1)

            def norm_out(k, place, uses):
                act.wait_ge(ln_tr, done(k + 1))
                act.wait_ge(xn_st[place], stored(uses))
                act.copy(xn_out[:, L * place:L * place + L].rearrange("p (x k) -> p x k", x=2), state_ps[:]).then_inc(ln_cp, 1)
                act.wait_ge(ln_cp, done(k + 1))
                act.dma_start(row(a["xn_scr"], k), xn_out[:, L * place:L * place + L].rearrange("p (k t) -> p k t", t=P)
                              ).then_inc(xn_st[place], DMA)

            def u_out(c, j, bank, u, used, stores, place):
                act.wait_ge(u_mm, done(j + 1))
                act.wait_ge(u_act, done(j))
                act.copy(v2(raw[:, TAPS - 1:]), hv(bank)).then_inc(u_raw, 1)
                act.wait_ge(wx_mm, done(used))
                act.wait_ge(u_st[place], stored(stores))
                act.activation(v2(u), hv(bank), ACT.Identity, bias=conv_b[:, bass.ds(c, 1)],
                               scale=conv_w[:, bass.ds(c * TAPS + TAPS - 1, 1)]).then_inc(u_tap, 1)

            def sigmoid(t, x, counter, at):
                act.activation(t, x, ACT.Exp, scale=-1.0).then_inc(counter, 1)
                act.wait_ge(counter, done(at + 1))
                act.activation(t, t, ACT.Ln, bias=consts[:, 2:3]).then_inc(counter, 1)
                act.wait_ge(counter, done(at + 2))
                act.activation(t, t, ACT.Exp, scale=-1.0).then_inc(counter, 1)

            def u_sigmoid(j, u):
                act.wait_ge(u_conv, done(3 * j + 3))
                sigmoid(raw[:, TAPS - 1:], u, u_sig, 3 * j)

            def softplus(step, c, place, i, y_used):
                bias = dt_bias[:, bass.ds(c, 1)]
                if step == 0:
                    act.wait_ge(dl_mm, done(i + 1))
                    act.wait_ge(du_ok, done(i - 1))
                    act.wait_ge(dl_add, done(i))
                    act.wait_ge(y_ok, done(y_used))
                    act.activation(v2(delta[:, place]), hv(g0), ACT.Relu, bias=bias).then_inc(dl_act, 1)
                    act.activation(v2(sp_tmp[:]), hv(g0), ACT.Abs, bias=bias).then_inc(dl_act, 1)
                elif step == 1:
                    act.wait_ge(dl_act, done(4 * i + 2))
                    act.activation(sp_tmp[:], sp_tmp[:], ACT.Exp, scale=-1.0).then_inc(dl_act, 1)
                else:
                    act.wait_ge(dl_act, done(4 * i + 3))
                    act.activation(sp_tmp[:], sp_tmp[:], ACT.Ln, bias=consts[:, 2:3]).then_inc(dl_act, 1)

            def gate(x, i):
                act.wait_ge(g_mm, done(2 * i + x + 1))
                act.wait_ge(y_ok, done(i))
                act.copy(s_gate[:, half(x)], g1[:, 0:HALF]).then_inc(g_act, 1)

            def gate_sigmoid(i, steps):
                act.wait_ge(g_act, done(2 * i + 2))
                act.wait_ge(dl_add, done(steps))
                sigmoid(sp_tmp[:], s_gate[:], g_sig, 3 * i)

            def ssm_root(b):
                act.wait_ge(rms_dve, done(RMS_STEPS * b + 6))
                act.activation(ssm_t[:], ssm_ms[:], ACT.Ln, bias=consts[:, 1:2]).then_inc(rms_root, 1)
                act.wait_ge(rms_root, done(2 * b + 1))
                act.activation(ssm_r[:], ssm_t[:], ACT.Exp, scale=-0.5).then_inc(rms_root, 1)

            def ssm_out(b):
                act.wait_ge(ssm_tr, done(b + 1))
                act.copy(ssmT[:, 0:4 * P], g0[0:RBC, 0, :]).then_inc(ssm_cp, 1)
                act.copy(ssmT[:, 4 * P:], g0[0:RBC, 1, 0:P]).then_inc(ssm_cp, 1)

            act.preload_act_table_set("natural_log_exp_and_others")
            act.wait_ge(setup, done(7))
            load_h(TT, TT % 2)
            load_h(TT + 1, (TT + 1) % 2)
            root(0)
            for t in range(TT):
                if t + 1 < TT:
                    root(t + 1)
                act.wait_ge(ln_tr, done(t + 1))
                act.copy(xnT[:, 0, :, P * t:P * t + P],
                         first_banks[t % 2][:].rearrange("p x (k t) -> p (x k) t", t=P)).then_inc(ln_cp, 1)

            act.wait_ge(cst_ld, DMA * 9)

            def first(c, place, c2, norm):
                k = c + TT
                u_out(c, c, first_banks[place], u_first_tiles[place], c - 1, c2, place)
                if norm:
                    root(k)
                u_sigmoid(c, u_first_tiles[place])
                if norm:
                    norm_out(k, 1 - place, c2)
                    if not isinstance(c, int) or k + 2 < B * TT:
                        load_h(k + 2, 1 - place)
            over_first(act, first)
            for s in range(2):
                act.wait_ge(xn_st[s], stored((B * TT - TT + s) // 2))
            ssm_root(0)
            ssm_out(0)
            for b in range(B):
                ahead = b + 1 < B
                for step in range(3):
                    softplus(step, 0, 0, DC * b, DC * b)

                def slot(c, place, c2, last, b=b, ahead=ahead):
                    i = c + DC * b
                    finish = ahead and last
                    for n in range(N):
                        k = N * i + n
                        if n == 0:
                            act.wait_ge(dl_add, done(i + 1))
                        act.wait_ge(scan_ok, done(2 * (k - RING_A + 1)))
                        act.activation(decay[:, n % RING_A], delta[:, place], ACT.Exp,
                                       scale=a_par[:, bass.ds(c * N + n, 1)]).then_inc(exp_ok, 1)
                        if n == (6 if finish else 8) and ahead:
                            u_out(c, i + DC, g0, u_new[:], i + DC, c2 + DC // 2 * (b + 1) + place, 1 - place)
                        if n == (9 if finish else 13):
                            gate(0, i)
                        if 12 <= n < 15 and not last:
                            softplus(n - 12, c + 1, 1 - place, i + 1, i)
                        if n == (11 if finish else 15) and ahead:
                            u_sigmoid(i + DC, u_new[:])
                        if n == 15 and finish:
                            ssm_root(b + 1)
                    gate(1, i)
                    gate_sigmoid(i, i + 1 if last else i + 2)
                    if finish:
                        ssm_out(b + 1)
                over_chunks(act, slot)

        @block.gpsimd
        def _(pool):
            def silu(j, u=u_new[:]):
                pool.wait_ge(u_sig, done(3 * j + 3))
                pool.tensor_tensor(u, u, raw[:, TAPS - 1:], ALU.mult).then_inc(u_act, 1)

            with pool.Fori(0, DC // 2) as c2:
                for place in range(2):
                    silu(2 * c2 + place, u_first_tiles[place])
            for b in range(B):
                ahead = b + 1 < B

                def slot(c, place, c2, last, b=b, ahead=ahead):
                    i = c + DC * b
                    finish = ahead and last
                    for n in range(N):
                        k = N * i + n
                        if n == 0:
                            pool.wait_ge(du_ok, done(i + 1))
                        if n in BC_FROM:
                            pool.wait_ge(bc_ld[BC_FROM.index(n)], 2 * DMA * (b + 1))
                        if n == 12 and finish:
                            silu(i + DC)
                        if n in own_steps(b):
                            continue
                        pool.wait_ge(scan_ok, done(2 * (k - RING_U + 1)))
                        pool.tensor_tensor(drive[:, n % RING_U], du[:, place], b_bc[:, n], ALU.mult).then_inc(drive_ok, 1)
                    if ahead and not last:
                        silu(i + DC)
                over_chunks(pool, slot)

        @block.vector
        def _(dve):
            def moments(k, place):
                for x in range(2):
                    dve.bn_stats(stats[:, 0 if place is None else place, x],
                                 h_at(k, place)[:, 512 * x:512 * x + 512]).then_inc(ln_bn, 1)
                dve.wait_ge(ln_bn, done(2 * k + 2))
                dve.wait_ge(ln_xn, done(k))
                dve.tensor_copy(carrier[:], stats[:, 0, 0, 0:1]).then_inc(ln_carried, 1)
                dve.bn_aggr(mv[:, 0:2], stats[:, 0 if place is None else place].rearrange("p x s -> p (x s)")).then_inc(ln_stat, 1)

            def normalize(k, place):
                dve.wait_ge(ln_root, done(2 * k + 2))
                newton_step(dve, mv[:, 1:2], mv[:, 2:3], mv[:, 3:4], LN_EPS, ln_newton, 4 * k)
                dve.tensor_scalar(h_at(k, place), h_at(k, place), mv[:, 0:1], mv[:, 2:3],
                                  ALU.subtract, ALU.mult).then_inc(ln_xn, 1)

            def conv(s, c, j, u=u_new[:]):
                if s == 0:
                    dve.wait_ge(u_raw, done(j + 1))
                    dve.wait_ge(u_tap, done(j + 1))
                else:
                    dve.wait_ge(u_conv, done(3 * j + s))
                lo = TAPS - 2 - s
                dve.scalar_tensor_tensor(out=u, in0=raw[:, lo:lo + TOK],
                                         scalar=conv_w[:, bass.ds(c * TAPS + TAPS - 2 - s, 1)], in1=u,
                                         op0=ALU.mult, op1=ALU.add).then_inc(u_conv, 1)

            def step_size(place, i, uses):
                dve.wait_ge(dl_act, done(4 * i + 4))
                dve.tensor_tensor(delta[:, place], delta[:, place], sp_tmp[:], ALU.add).then_inc(dl_add, 1)
                dve.wait_ge(dl_add, done(i + 1))
                dve.wait_ge(uy_ld[place], DMA * uses)
                dve.tensor_tensor(du[:, place], delta[:, place], u_y[:, place], ALU.mult).then_inc(du_ok, 1)

            parts = ((0, R), (R, R + N), (R + N, RBC))

            def ssm_squares(b):
                at = RMS_STEPS * b
                dve.wait_ge(wx_mm, done(DC * (b + 1)))
                dve.tensor_copy(ssm[:].rearrange("p t r -> p (t r)"), ssm_ps[:, 0:TT * RBC]).then_inc(rms_dve, 1)
                dve.wait_ge(rms_dve, done(at + 1))
                dve.wait_ge(ln_tr, done(TT * B))
                sq = h_t[:, 0, 0:TT * RBC].rearrange("p (t r) -> p t r", r=RBC)
                dve.tensor_tensor(sq, ssm[:], ssm[:], ALU.mult).then_inc(rms_dve, 1)
                dve.wait_ge(rms_dve, done(at + 2))
                for x, (lo, hi) in enumerate(parts):
                    dve.tensor_reduce(ssm_ms[:, x], sq[:, :, lo:hi], AX, ALU.add).then_inc(rms_dve, 1)
                dve.wait_ge(rms_dve, done(at + 5))
                dve.tensor_tensor(ssm_ms[:], ssm_ms[:], inv_count[:], ALU.mult).then_inc(rms_dve, 1)

            def ssm_scale(b):
                at = RMS_STEPS * b
                dve.wait_ge(rms_root, done(2 * b + 2))
                newton_step(dve, ssm_ms[:], ssm_r[:], ssm_t[:], RMS_EPS, rms_dve, at + 6)
                for x, (lo, hi) in enumerate(parts):
                    dve.tensor_tensor(ssm[:, :, lo:hi], ssm[:, :, lo:hi],
                                      ssm_r[:, x].unsqueeze(2).broadcast_to([P, TT, hi - lo]), ALU.mult).then_inc(rms_dve, 1)
                dve.wait_ge(rms_dve, done(at + 13))
                dve.tensor_tensor(ssm[:], ssm[:], ln_w[:].unsqueeze(1).broadcast_to([P, TT, RBC]), ALU.mult).then_inc(rms_dve, 1)

            dve.memset(consts[:, 0:1], LN_EPS).then_inc(setup, 1)
            dve.memset(consts[:, 1:2], RMS_EPS).then_inc(setup, 1)
            dve.memset(consts[:, 2:3], 1.0).then_inc(setup, 1)
            dve.memset(inv_count[:, 0], 1.0 / R).then_inc(setup, 1)
            dve.memset(inv_count[:, 1:3], 1.0 / N).then_inc(setup, 1)
            dve.memset(zero[:], 0.0).then_inc(setup, 1)
            dve.memset(raw[:, 0:TAPS - 1], 0.0).then_inc(setup, 1)
            dve.wait_ge(setup, done(7))
            for t in range(TT):
                dve.wait_ge(h0_ld[t], DMA)
                moments(t, None)
                normalize(t, None)

            dve.wait_ge(cst_ld, DMA * 9)

            def first(c, place, c2, norm):
                k = c + TT
                if norm:
                    dve.wait_ge(ht_ld[1 - place], DMA * (c2 + 1))
                    moments(k, 1 - place)
                for s in range(TAPS - 1):
                    conv(s, c, c, u_first_tiles[place])
                if norm:
                    normalize(k, 1 - place)
            over_first(dve, first)
            ssm_squares(0)
            ssm_scale(0)
            dve.wait_ge(u_st[1], stored(DC // 2))
            for b in range(B):
                ahead = b + 1 < B
                step_size(0, DC * b, DC // 2 * b + 1)

                def slot(c, place, c2, last, b=b, ahead=ahead):
                    i = c + DC * b
                    finish = ahead and last
                    def scan(h):
                        n, x = h // 2, h % 2
                        at = 2 * N * i + h
                        if x:
                            dve.wait_ge(scan_ok, done(at))
                        dve.wait_ge(prod_ok, done(at - h if h < STATES else at - STATES + 1))
                        dve.tensor_tensor_scan(states[:, h % STATES], decay[:, n % RING_A, half(x)], drive[:, n % RING_U, half(x)],
                                               states[:, (h - 1) % STATES, HALF - 1:HALF] if x else 0.0,
                                               ALU.mult, ALU.add).then_inc(scan_ok, 1)

                    def product(h):
                        n, x = h // 2, h % 2
                        dve.wait_ge(scan_ok, done(2 * N * i + h + 1))
                        if x == 0:
                            dve.wait_ge(sum_ok, done(N * i + n - RING_C + 1))
                        dve.tensor_tensor(prod[:, n % RING_C, half(x)], states[:, h % STATES], c_bc[:, n, half(x)],
                                          ALU.mult).then_inc(prod_ok, 1)

                    for n in range(N):
                        k = N * i + n
                        s0 = n - (6 if finish else 9)
                        if 0 <= s0 < 3 and ahead:
                            conv(s0, c, i + DC)
                        if n == 13 and finish:
                            ssm_squares(b + 1)
                        if n == 15 and finish:
                            ssm_scale(b + 1)
                        if n in BC_FROM:
                            dve.wait_ge(bc_ld[BC_FROM.index(n)], 2 * DMA * (b + 1))
                        if n in own_steps(b):
                            dve.wait_ge(drive_own, done(own_drives(b, c, n)))
                        else:
                            dve.wait_ge(drive_ok, done(pool_drives(b, c, n)))
                        dve.wait_ge(exp_ok, done(k + 1))
                        scan(2 * n)
                        if n:
                            product(2 * n - 1)
                        scan(2 * n + 1)
                        m = n + 1
                        if m in own_steps(b):
                            dve.wait_ge(scan_ok, done(2 * (N * i + m - RING_U + 1)))
                            dve.tensor_tensor(drive[:, m % RING_U], du[:, place], b_bc[:, m], ALU.mult).then_inc(drive_own, 1)
                        product(2 * n)
                    product(2 * N - 1)
                    if not last:
                        step_size(1 - place, i + 1, c2 + (DC // 2 * b + 1 + place))
                    dve.wait_ge(sum_ok, done(N * i + N))
                    dve.scalar_tensor_tensor(out=v2(u_y[:, place]), in0=v2(u_y[:, place]), scalar=d_par[:, bass.ds(c, 1)],
                                             in1=hv(y_ps), op0=ALU.mult, op1=ALU.add).then_inc(y_half, 1)
                    dve.wait_ge(g_sig, done(3 * i + 3))
                    dve.tensor_tensor(s_gate[:], s_gate[:], sp_tmp[:], ALU.mult).then_inc(y_gate, 1)
                    dve.wait_ge(y_gate, done(i + 1))
                    dve.wait_ge(y_half, done(i + 1))
                    dve.tensor_tensor(u_y[:, place], u_y[:, place], s_gate[:], ALU.mult).then_inc(y_ok, 1)
                over_chunks(dve, slot)

        @block.tensor
        def _(pe):
            def norm_transpose(k, place, bank):
                pe.wait_ge(ln_xn, done(k + 1))
                for m in range(KC):
                    last = pe.transpose(bank[:, m // 4, P * (m % 4):P * (m % 4) + P], h_at(k, place)[:, P * m:P * m + P], ident[:])
                last.then_inc(ln_tr, 1)

            def u_step(m, place, bank, xn):
                for x in range(2):
                    last = pe.matmul(bank[:, x, 0:HALF], w_u[:, place, m, :], xnT[:, xn, m, half(x)],
                                     start=(m == 0), stop=(m == KC - 1))
                if m == KC - 1:
                    last.then_inc(u_mm, 1)

            def u_first(place, c, uses):
                pe.wait_ge(wu_ld[place], DMA * uses)
                pe.wait_ge(u_tap, done(c - 1))
                for m in range(KC):
                    u_step(m, place, first_banks[place], 0)

            def gate_step(s, place, xn):
                x = s // (KC // 2)
                for m in (2 * s % KC, 2 * s % KC + 1):
                    last = pe.matmul(g1[:, 0:HALF], w_g[:, place, m, :], xnT[:, xn, m, half(x)],
                                     start=(m == 0), stop=(m == KC - 1))
                if m == KC - 1:
                    last.then_inc(g_mm, 1)

            def clear_ssm():
                pe.matmul(ssm_ps[:, 0:TT * RBC], zero[:], w_x[0:1, 0:TT * RBC], start=True, stop=False, skip_group_check=True)

            def wx(c, j, u=u_new):
                pe.wait_ge(u_act, done(j + 1))
                for t in range(TT):
                    last = pe.matmul(ssm_ps[:, RBC * t:RBC * t + RBC], u[:, P * t:P * t + P], w_x[:, bass.ds(c * RBC, RBC)],
                                     start=False, stop=False, skip_group_check=True)
                last.then_inc(wx_mm, 1)

            def ssm_transpose(b):
                pe.wait_ge(rms_dve, done(RMS_STEPS * (b + 1)))
                pe.wait_ge(u_tap, done(DC * (b + 1)))
                for t in range(TT):
                    last = pe.transpose(g0[0:RBC, t // 4, P * (t % 4):P * (t % 4) + P], ssm[:, t, :], ident[:])
                last.then_inc(ssm_tr, 1)

            def step_product(place, i, uses):
                pe.wait_ge(wdt_ld[place], DMA * uses)
                for x in range(2):
                    last = pe.matmul(g0[:, x, 0:HALF], w_dt[:, place, :], ssmT[0:R, half(x)], start=True, stop=True)
                last.then_inc(dl_mm, 1)

            pe.wait_ge(id_ld, DMA)
            pe.wait_ge(setup, done(7))
            for t in range(TT):
                pe.wait_ge(ln_cp, done(t - 1))
                norm_transpose(t, None, first_banks[t % 2])
            pe.wait_ge(cst_ld, DMA * 9)
            clear_ssm()
            pe.wait_ge(ln_cp, done(TT))
            u_first(0, 0, 1)

            def first(c, place, c2, norm):
                if not isinstance(c, int) or c + 1 < DC:
                    u_first(1 - place, c + 1, c2 + 1 + place)
                if norm:
                    pe.wait_ge(ln_cp, done(c + TT))
                    norm_transpose(c + TT, 1 - place, state_ps)
                wx(c, c, u_first_tiles[place])
            over_first(pe, first)
            ssm_transpose(0)
            for b in range(B):
                ahead = b + 1 < B
                pe.wait_ge(ssm_cp, done(2 * (b + 1)))
                step_product(0, DC * b, DC // 2 * b + 1)
                if ahead:
                    pe.wait_ge(rms_dve, done(RMS_STEPS * b + 1))
                    clear_ssm()
                    pe.wait_ge(xn_ld, TT * DMA * (b + 1))

                def slot(c, place, c2, last, b=b, ahead=ahead):
                    i = c + DC * b
                    j = i + DC
                    finish = ahead and last
                    for n in range(N):
                        k = N * i + n
                        if n == 0 and ahead:
                            pe.wait_ge(wu_ld[place], DMA * (c2 + (DC // 2 * (b + 1) + 1)))
                            pe.wait_ge(dl_act, done(4 * i + 4))
                        if ahead:
                            for m in ((2 * n, 2 * n + 1) if finish else range(3) if n == 0 else (n + 2,)):
                                if m < KC:
                                    u_step(m, place, g0, (b + 1) % 2)
                        g = n - (4 if finish else 6)
                        if g == 0:
                            pe.wait_ge(wg_ld[place], DMA * (c2 + (DC // 2 * b + 1)))
                            pe.wait_ge(g_act, done(2 * i))
                        if g == KC // 2:
                            pe.wait_ge(g_act, done(2 * i + 1))
                        if 0 <= g < KC:
                            gate_step(g, place, b % 2)
                        if n == 8 and not last:
                            if ahead:
                                pe.wait_ge(u_tap, done(j + 1))
                            else:
                                pe.wait_ge(dl_act, done(4 * i + 4))
                            step_product(1 - place, i + 1, c2 + (DC // 2 * b + 1 + place))
                        if n == 12 and finish:
                            wx(c, j)
                        if n == 0:
                            pe.wait_ge(y_half, done(i))
                        for x in range(2):
                            pe.wait_ge(prod_ok, done(2 * k + x + 1))
                            mm = pe.matmul(y_ps[:, x, 0:HALF], ident[:], prod[:, n % RING_C, half(x)],
                                           start=(n == 0), stop=(n == N - 1))
                        mm.then_inc(sum_ok, 1)
                    if ahead and not last:
                        wx(c, j)
                    if finish:
                        ssm_transpose(b + 1)
                over_chunks(pe, slot)


def output_part(nc, a, sem):
    TILES = B * TT
    with ExitStack() as ctx:
        sb = lambda name, shape: ctx.enter_context(nc.sbuf_tensor(name, shape, F32))
        pair = lambda name: [sem(f"{name}{x}") for x in range(2)]
        split = lambda name, shape: [ctx.enter_context(nc.sbuf_tensor(f"{name}_{x}", shape, F32R)) for x in ("hi", "lo")]
        w_hi, w_lo = split("w_out", [P, DC, L])
        w_a, w_b = sb("w_a_sb", [P, KC, BN]), sb("w_b_sb", [P, MC, L])
        w_q, keys = sb("w_q_sb", [P, KC, RD]), sb("keys_sb", [RD, E])
        ident = sb("o_ident", [P, P])
        y_raw = sb("y_raw", [P, DC, P])
        y_hi, y_lo = split("y", [P, DC, P])
        h = sb("o_h", [P, 2, L])
        xn = sb("o_xn", [P, L])
        xnT = sb("o_xnT", [P, KC, P])
        stage = (h[:, 1], xn[:], xnT[:].rearrange("p k t -> p (k t)"))
        zg, zgT = sb("zg", [P, BN]), sb("zgT", [P, MC, P])
        qT = sb("qT", [RD, P])
        score, left, ex = sb("score", [P, E]), sb("left", [P, 2, E]), sb("ex", [P, E])
        top = sb("top", [P, 2, 8])
        carrier = sb("carrier", [P, 5])
        scal = sb("scal", [P, 4])
        stats, mv, eps = sb("o_stats", [P, 2, 6]), sb("o_mv", [P, 4]), sb("o_eps", [P, 1])
        psum = lambda name, shape: ctx.enter_context(nc.psum_tensor(name, shape, F32))
        o_ps, t_ps, f_ps = psum("o_ps", [P, L]), psum("t_ps", [P, L]), psum("f_ps", [P, L])
        z_ps, s_ps = psum("z_ps", [P, BN]), psum("s_ps", [P, 512])

        ld, wb_ld, y_ld, h_ld, out_st = sem("o_ld"), sem("wb_ld"), sem("y_ld"), pair("h_ld"), pair("out_st")
        stage_ld = [sem(f"stage_ld{x}") for x in range(len(stage))]
        names = ("o_setup w_hi_ok w_lo_ok y_hi_ok y_lo_ok o_mm h2_half h2_ok o_bn o_stat o_root o_newton xn_ok xt_mm xt_cp q_mm q_cp z_mm s_mm "
                 "carried sel sel_r sel_exp zg_ok zt_mm zt_cp f_mm out_ok").split()
        counters = [sem(n) for n in names]
        (o_setup, w_hi_ok, w_lo_ok, y_hi_ok, y_lo_ok, o_mm, h2_half, h2_ok, o_bn, o_stat, o_root, o_newton, xn_ok, xt_mm, xt_cp, q_mm, q_cp, z_mm, s_mm,
         carried, sel, sel_r, sel_exp, zg_ok, zt_mm, zt_cp, f_mm, out_ok) = counters
        with nc.Block() as credits:
            @credits.gpsimd
            def _(pool):
                for s in counters:
                    pool.sem_inc(s, CREDIT)
                for s in out_st:
                    pool.sem_inc(s, DMA)
        block = ctx.enter_context(nc.Block())
        SEL = 9

        def over_tiles(eng, body):
            with eng.Fori(0, TILES // 2 - 1) as q2:
                for place in range(2):
                    body(2 * q2 + place, place, q2, False)
            for place in range(2):
                body(TILES - 2 + place, place, TILES // 2 - 1, place == 1)

        @block.sync
        def _(sp):
            def load(q):
                sp.wait_ge(y_lo_ok, done(q))
                sp.dma_start(y_raw[:], row(a["y_scr"], q)).then_inc(y_ld, DMA)

            def load_h(q, place, uses):
                sp.wait_ge(out_st[place], stored(uses))
                sp.dma_start(h[:, place], row(a["h_rows"], q)).then_inc(h_ld[place], DMA)

            load(0)
            sp.dma_start(ident[:], a["ident"]).then_inc(ld, DMA)
            for c in range(DC):
                if c == len(stage):
                    load_h(0, 0, 0)
                sp.wait_ge(w_lo_ok, done(c - len(stage) + 1))
                sp.dma_start(stage[c % len(stage)], a["w_out"][:, c, :]).then_inc(stage_ld[c % len(stage)], DMA)
            for dst, src in ((w_q[:], a["w_q"]), (w_a[:], a["w_a"]), (keys[:], a["keysT"])):
                sp.dma_start(dst, src).then_inc(ld, DMA)
            sp.dma_start(w_b[:], a["w_b"]).then_inc(wb_ld, DMA)
            load(1)
            sp.wait_ge(w_lo_ok, done(DC))

            def tile(q, place, q2, last):
                if not last:
                    if not isinstance(q, int):
                        load(q + 2)
                    load_h(q + 1, 1 - place, q2 if place == 0 else q2 + 1)
                sp.wait_ge(out_ok, done(q + 1))
                sp.dma_start(row(a["out"], q), h[:, place]).then_inc(out_st[place], DMA)
            over_tiles(sp, tile)
            for s in out_st:
                sp.wait_ge(s, stored(TILES // 2))

        @block.tensor
        def _(pe):
            def project(q, weights, middle):
                pe.wait_ge(y_lo_ok, done(q + 1))
                pe.wait_ge(h2_ok, done(q))
                for c in range(DC):
                    weights(c)
                    if c == DC // 2:
                        middle()
                    for y, w in ((y_hi, w_hi), (y_hi, w_lo), (y_lo, w_hi)):
                        for x in range(2):
                            last = pe.matmul(o_ps[:, 512 * x:512 * x + 512], y[:, c, :], w[:, c, 512 * x:512 * x + 512],
                                             start=(c == 0 and w is w_hi and y is y_hi), stop=(c == DC - 1 and y is y_lo))
                last.then_inc(o_mm, 1)

            def gated_transposes(q):
                pe.wait_ge(zg_ok, done(q + 1))
                for m in range(MC):
                    mm = pe.transpose(t_ps[:, P * m:P * m + P], zg[:, P * m:P * m + P], ident[:])
                mm.then_inc(zt_mm, 1)

            project(0, lambda c: pe.wait_ge(w_lo_ok, done(c + 1)), lambda: None)
            pe.wait_ge(ld, DMA * 4)

            def tile(q, place, q2, last):
                pe.wait_ge(xn_ok, done(q + 1))
                pe.wait_ge(zt_cp, done(q))
                for m in range(KC):
                    mm = pe.transpose(t_ps[:, P * m:P * m + P], xn[:, P * m:P * m + P], ident[:])
                    if m % (KC // 2) == KC // 2 - 1:
                        mm.then_inc(xt_mm, 1)
                for m in range(KC):
                    if m % (KC // 2) == 0:
                        pe.wait_ge(xt_cp, done(2 * q + 1 + m // (KC // 2)))
                    mm = pe.matmul(s_ps[0:RD, 0:P], w_q[:, m, :], xnT[:, m, :], start=(m == 0), stop=(m == KC - 1))
                mm.then_inc(q_mm, 1)
                pe.wait_ge(zg_ok, done(q))
                for m in range(KC):
                    mm = pe.matmul(z_ps[:], xnT[:, m, :], w_a[:, m, :], start=(m == 0), stop=(m == KC - 1))
                mm.then_inc(z_mm, 1)
                pe.wait_ge(q_cp, done(q + 1))
                pe.matmul(s_ps[:, P:P + E], qT[:], keys[:], start=True, stop=True).then_inc(s_mm, 1)
                if last:
                    gated_transposes(q)
                else:
                    project(q + 1, lambda c: None, lambda: gated_transposes(q))
                pe.wait_ge(zt_cp, done(q + 1))
                pe.wait_ge(out_ok, done(q))
                pe.wait_ge(wb_ld, DMA)
                for m in range(MC):
                    for x in range(2):
                        mm = pe.matmul(f_ps[:, 512 * x:512 * x + 512], zgT[:, m, :], w_b[:, m, 512 * x:512 * x + 512],
                                       start=(m == 0), stop=(m == MC - 1))
                mm.then_inc(f_mm, 1)
            over_tiles(pe, tile)

        @block.scalar
        def _(act):
            def root(q):
                act.wait_ge(o_stat, done(q + 1))
                act.activation(mv[:, 2:3], mv[:, 1:2], ACT.Ln, bias=eps[:]).then_inc(o_root, 1)
                act.wait_ge(o_root, done(2 * q + 1))
                act.activation(mv[:, 3:4], mv[:, 2:3], ACT.Exp, scale=-0.5).then_inc(o_root, 1)

            act.preload_act_table_set("natural_log_exp_and_others")
            act.wait_ge(o_setup, done(1))

            def split_y(q):
                act.wait_ge(y_ld, DMA * (q + 1))
                act.wait_ge(o_mm, done(q))
                act.copy(y_hi[:], y_raw[:]).then_inc(y_hi_ok, 1)

            split_y(0)
            for c in range(DC):
                act.wait_ge(stage_ld[c % len(stage)], DMA * (c // len(stage) + 1))
                act.copy(w_hi[:, c], stage[c % len(stage)]).then_inc(w_hi_ok, 1)
            root(0)

            def tile(q, place, q2, last):
                if not last:
                    split_y(q + 1)
                act.wait_ge(z_mm, done(q))
                for x in range(2):
                    act.wait_ge(xt_mm, done(2 * q + x + 1))
                    act.copy(xnT[:, KC // 2 * x:KC // 2 * (x + 1)].rearrange("p k t -> p (k t)"),
                             t_ps[:, 512 * x:512 * x + 512]).then_inc(xt_cp, 1)
                act.wait_ge(q_mm, done(q + 1))
                act.copy(qT[:], s_ps[0:RD, 0:P]).then_inc(q_cp, 1)
                act.wait_ge(sel, done(SEL * q + 3))
                act.activation(ex[:], score[:], ACT.Exp, bias=scal[:, 0:1]).then_inc(sel_exp, 1)
                act.wait_ge(zt_mm, done(q + 1))
                act.wait_ge(f_mm, done(q))
                act.copy(zgT[:].rearrange("p m t -> p (m t)"), t_ps[:, 0:BN]).then_inc(zt_cp, 1)
                if not last:
                    root(q + 1)
            over_tiles(act, tile)

        @block.vector
        def _(dve):
            def front(q, place, uses):
                dve.wait_ge(o_mm, done(q + 1))
                dve.wait_ge(h_ld[place], DMA * uses)
                dve.tensor_tensor(h[:, place], h[:, place], o_ps[:], ALU.add).then_inc(h2_ok, 1)
                dve.wait_ge(h2_ok, done(q + 1))
                for x in range(2):
                    dve.bn_stats(stats[:, x], h[:, place, 512 * x:512 * x + 512]).then_inc(o_bn, 1)
                dve.wait_ge(o_bn, done(2 * q + 2))
                dve.tensor_copy(carrier[:, 0:1], stats[:, 0, 0:1]).then_inc(carried, 1)
                dve.bn_aggr(mv[:, 0:2], stats[:].rearrange("p x s -> p (x s)")).then_inc(o_stat, 1)
                dve.wait_ge(o_root, done(2 * q + 2))
                newton_step(dve, mv[:, 1:2], mv[:, 3:4], mv[:, 2:3], LN_EPS, o_newton, 4 * q)
                dve.wait_ge(xt_mm, done(2 * q))
                dve.tensor_scalar(xn[:], h[:, place], mv[:, 0:1], mv[:, 3:4], ALU.subtract, ALU.mult).then_inc(xn_ok, 1)

            dve.memset(eps[:], LN_EPS).then_inc(o_setup, 1)

            def split_y(q):
                dve.wait_ge(y_hi_ok, done(q + 1))
                dve.wait_ge(o_mm, done(q))
                dve.tensor_tensor(y_lo[:], y_raw[:], y_hi[:].bitcast(F32), ALU.subtract).then_inc(y_lo_ok, 1)

            split_y(0)
            for c in range(DC):
                dve.wait_ge(w_hi_ok, done(c + 1))
                dve.tensor_tensor(w_lo[:, c], stage[c % len(stage)], w_hi[:, c].bitcast(F32), ALU.subtract).then_inc(w_lo_ok, 1)
            front(0, 0, 1)

            def tile(q, place, q2, last):
                if not last:
                    split_y(q + 1)
                at = q * SEL

                def link(step, ins):
                    ins.then_inc(sel, 1)
                    dve.wait_ge(sel, done(at + step))

                dve.wait_ge(s_mm, done(q + 1))
                link(1, dve.tensor_copy(score[:], s_ps[:, P:P + E]))
                dve.tensor_copy(carrier[:, 1:2], score[:, 0:1]).then_inc(carried, 1)
                link(2, dve.max(top[:, 0], score[:]))
                link(3, dve.tensor_scalar(scal[:, 0:1], top[:, 0, 0:1], -1.0, None, ALU.mult))
                dve.tensor_copy(carrier[:, 2:3], scal[:, 0:1]).then_inc(carried, 1)
                link(4, dve.match_replace(left[:, 0], top[:, 0], score[:], -3.0e38))
                dve.tensor_copy(carrier[:, 3:4], left[:, 0, 0:1]).then_inc(carried, 1)
                link(5, dve.max(top[:, 1], left[:, 0]))
                dve.tensor_copy(carrier[:, 4:5], top[:, 1, 0:1]).then_inc(carried, 1)
                link(6, dve.match_replace(left[:, 1], top[:, 1], left[:, 0], -3.0e38))
                link(7, dve.tensor_tensor(left[:, 0], score[:], left[:, 1], ALU.not_equal))
                dve.wait_ge(sel_exp, done(q + 1))
                link(8, dve.tensor_tensor(ex[:], ex[:], left[:, 0], ALU.mult))
                dve.tensor_reduce(scal[:, 1:2], ex[:], AX, ALU.add).then_inc(sel, 1)
                dve.wait_ge(sel, done(at + 9))
                dve.reciprocal(scal[:, 2:3], scal[:, 1:2]).then_inc(sel_r, 1)
                dve.wait_ge(sel_r, done(2 * q + 1))
                dve.tensor_scalar(ex[:], ex[:], scal[:, 2:3], 2.0, ALU.mult, ALU.mult).then_inc(sel_r, 1)
                dve.wait_ge(sel_r, done(2 * q + 2))
                dve.wait_ge(z_mm, done(q + 1))
                dve.wait_ge(zt_mm, done(q))
                dve.tensor_tensor(zg[:].rearrange("p (e r) -> p e r", e=E), z_ps[:].rearrange("p (e r) -> p e r", e=E),
                                  ex[:].unsqueeze(2).broadcast_to([P, E, RANK]), ALU.mult).then_inc(zg_ok, 1)
                if not last:
                    front(q + 1, 1 - place, (q2 + 1) if place == 0 else (q2 + 2))
                dve.wait_ge(f_mm, done(q + 1))
                dve.tensor_tensor(h[:, place], h[:, place], f_ps[:], ALU.add).then_inc(out_ok, 1)
            over_tiles(dve, tile)


def build(nc, a):
    with ExitStack() as ctx:
        sem = lambda name: ctx.enter_context(nc.semaphore(name))
        tokens_part(nc, a, sem)
        mixer_part(nc, a, sem)
        output_part(nc, a, sem)


def constants():
    t = np.zeros((P, NV + 4), np.float32)
    t[:, 0:NA] = 64 * np.arange(NA)
    t[:, NA:NA + NB1] = NB2 * np.arange(NB1)
    t[:, NA + NB1:NV] = np.arange(NB2)
    re = np.arange(P) < 64
    t[:, NV] = np.where(re, 0.25, 0)
    t[:, NV + 1] = np.where(re, np.pi / 2, 0)
    t[:, NV + 2] = np.where(re, 1, -1)
    t[:, NV + 3] = -t[:, NV + 2]
    return t


def layouts(x):
    cont = np.ascontiguousarray
    per_chunk = lambda v, w: cont(v.reshape(DC, P, w).transpose(1, 0, 2).reshape(P, DC * w))
    lhs = lambda w: cont(w.reshape(DC, P, KC, P).transpose(0, 3, 2, 1))
    rhs = lambda w, k: cont(w.T.reshape(k, P, w.shape[0]).transpose(1, 0, 2))
    s4, w_in = x["x"], x["L0_attn_W_in"]
    return {
        "aimT": cont(x["L0_tok_A_imag"].T), "iarT": cont(x["L0_tok_inv_A_real"].T),
        "brT": cont(x["L0_tok_B"][..., 0].T), "biT": cont(x["L0_tok_B"][..., 1].T),
        "crT": cont(s4[..., 0].transpose(2, 0, 1)), "ciT": cont(s4[..., 1].transpose(2, 0, 1)),
        "log_dt": x["L0_tok_log_dt"], "txt": x["txt"],
        "w_u": lhs(w_in[:D]), "w_g": lhs(w_in[D:]),
        "w_dt": cont(x["L0_attn_Wdt"].reshape(DC, P, R).transpose(0, 2, 1)),
        "w_x": rhs(x["L0_attn_Wx"], DC).reshape(P, DC * RBC),
        "A": per_chunk(x["L0_attn_A"], N), "conv_w": per_chunk(x["L0_attn_conv_w"], TAPS),
        "conv_b": per_chunk(x["L0_attn_conv_b"], 1), "dt_bias": per_chunk(x["L0_attn_dt_bias"], 1),
        "D": per_chunk(x["L0_attn_D_param"], 1),
        "dt_ln": x["L0_attn_dt_ln_w"], "b_ln": x["L0_attn_b_ln_w"], "c_ln": x["L0_attn_c_ln_w"],
        "w_out": rhs(x["L0_attn_W_out"], DC), "w_a": rhs(x["L0_ffn_A_w"], KC), "w_b": rhs(x["L0_ffn_B_w"], MC),
        "w_q": rhs(x["L0_ffn_Wq_w"], KC), "keysT": cont(x["L0_ffn_keys"].T),
        "cst": constants(), "ident": np.eye(P, dtype=np.float32),
    }


def kernel(**inputs):
    import concourse.bacc as bacc
    from concourse.bass_utils import run_bass_kernel_spmd

    nc = bacc.Bacc("TRN2", target_bir_lowering=False, num_devices=1)
    arrays = layouts({k: np.asarray(v) for k, v in inputs.items()})
    a = {k: nc.dram_tensor(f"in_{k}", v.shape, F32, kind="ExternalInput").ap() for k, v in arrays.items()}
    for name, shape in (("h_all", [B, TOK, L]), ("u_scr", [B * DC, P, TOK]), ("y_scr", [B * TT, P, DC, P]),
                        ("bc_scr", [B, 2 * N, TOK]), ("xn_scr", [B * TT, P, KC, P])):
        a[name] = nc.dram_tensor(name, shape, F32, kind="Internal").ap()
    out = nc.dram_tensor("out", [B, TOK, L], F32, kind="ExternalOutput").ap()
    tiles = lambda t: t.rearrange("b (t p) l -> (b t) p l", p=P)
    a["h_rows"], a["out"] = tiles(a["h_all"]), tiles(out)
    build(nc, a)
    r = run_bass_kernel_spmd(nc, [{f"in_{k}": v for k, v in arrays.items()}], core_ids=[0])
    return r.results[0]["out"]
```
